# Optimizing a Trainium2 kernel written in Bass

```python
import numpy as np
import jax
import jax.numpy as jnp

def _softmax(x, axis=-1):
    return jax.nn.softmax(x, axis=axis)

def _gelu(x):
    return jax.nn.gelu(x, approximate=True)

def _silu(x):
    return jax.nn.silu(x)

def _sigmoid(x):
    return jax.nn.sigmoid(x)

def _layernorm(x, axis=-1, eps=1e-05):
    m = jnp.mean(x, axis=axis, keepdims=True)
    v = jnp.var(x, axis=axis, keepdims=True)
    return (x - m) / jnp.sqrt(v + eps)

def _scatter_add(tgt, idx, src, axis=0):
    return tgt.at[idx].add(src)

def _segment_sum(src, seg, n):
    return jax.ops.segment_sum(src, seg, n)
kernel_name = 'mk_adj_ffn_d1_adj_r2_c216e0'

def setup_inputs(seed: int=0):
    np.random.seed(seed)
    _w = jnp.asarray

    def _rec_inputs():
        import jax
        import jax.numpy as jnp
        _gk = jax.random.key(seed)
        x = -0.0002928 + 1 * jax.random.normal(jax.random.fold_in(_gk, 1), (2048, 256), jnp.float32)
        _a = jax.random.bernoulli(jax.random.fold_in(_gk, 2), 0.00195312, (2048, 2048))
        _a = jnp.logical_or(_a, jnp.eye(2048, dtype=bool))
        _af = _a.astype(jnp.float32)
        _af = _af * jax.random.uniform(jax.random.fold_in(_gk, 3), (2048, 2048), jnp.float32, 0.05, 1)
        adj = _af
        return (x, adj)
    x, adj = _rec_inputs()

    def _L0_gnn_setup():
        import jax, jax.numpy as jnp
        import numpy as np
        N = 4096
        D = 256
        key = jax.random.key(seed)
        k1, k2 = jax.random.split(key)
        inp = jax.random.normal(k1, (N, D), dtype=jnp.float32)
        A = jax.random.uniform(k2, (N, N), dtype=jnp.float32)
        W = jnp.ones((D,), dtype=jnp.float32)
        return {'input': inp, 'A': A, 'W': W}
    _L0_gnn_all = _L0_gnn_setup()
    _L0_gnn_in = {k: v for k, v in _L0_gnn_all.items() if k in ('W',)}
    del _L0_gnn_all

    def _L0_ffn_setup():
        import jax, jax.numpy as jnp
        import numpy as np
        D_MODEL, D_STATE, D_CONV, D_INPUT, D_OUTPUT = (512, 16, 4, 256, 256)
        EXPAND = 2
        D_INNER = EXPAND * D_MODEL
        DT_RANK = (D_MODEL + 15) // 16
        B, L = (4, 1024)

        def _mamba(x, W_in, conv_w, conv_b, W_xproj, W_dt, b_dt, A_log, Dp, W_out):
            xz = jnp.einsum('bld,ed->ble', x, W_in)
            u, z = jnp.split(xz, 2, axis=-1)
            u_pad = jnp.pad(u, ((0, 0), (D_CONV - 1, 0), (0, 0)))
            u = sum((u_pad[:, k:k + u.shape[1], :] * conv_w[:, k] for k in range(D_CONV))) + conv_b
            u = jax.nn.silu(u)
            dbc = jnp.einsum('bld,ed->ble', u, W_xproj)
            dt, B_ssm, C_ssm = jnp.split(dbc, [DT_RANK, DT_RANK + D_STATE], axis=-1)
            delta = jax.nn.softplus(jnp.einsum('blr,dr->bld', dt, W_dt) + b_dt)
            A = -jnp.exp(A_log)

            def step(h, ins):
                d_t, B_t, C_t, u_t = ins
                dA = jnp.exp(d_t[..., None] * A)
                h = dA * h + (d_t * u_t)[..., None] * B_t[:, None, :]
                y_t = jnp.einsum('bds,bs->bd', h, C_t)
                return (h, y_t)
            h0 = jnp.zeros((u.shape[0], D_INNER, D_STATE), u.dtype)
            xs = (delta.transpose(1, 0, 2), B_ssm.transpose(1, 0, 2), C_ssm.transpose(1, 0, 2), u.transpose(1, 0, 2))
            _, y = jax.lax.scan(step, h0, xs)
            y = y.transpose(1, 0, 2) + u * Dp
            y = y * jax.nn.silu(z)
            return jnp.einsum('bld,ed->ble', y, W_out)
        key = jax.random.key(seed)
        ks = jax.random.split(key, 16)
        s = lambda fan_in: 1.0 / np.sqrt(fan_in)
        inp = {'x': jax.random.normal(ks[0], (B, L, D_INPUT), jnp.float32), 'W_fc1': jax.random.normal(ks[1], (D_MODEL, D_INPUT), jnp.float32) * s(D_INPUT), 'b_fc1': jnp.zeros((D_MODEL,), jnp.float32), 'W_in': jax.random.normal(ks[2], (2 * D_INNER, D_MODEL), jnp.float32) * s(D_MODEL), 'conv_w': jax.random.normal(ks[3], (D_INNER, D_CONV), jnp.float32) * s(D_CONV), 'conv_b': jnp.zeros((D_INNER,), jnp.float32), 'W_xproj': jax.random.normal(ks[4], (DT_RANK + 2 * D_STATE, D_INNER), jnp.float32) * s(D_INNER), 'W_dt': jax.random.normal(ks[5], (D_INNER, DT_RANK), jnp.float32) * s(DT_RANK), 'b_dt': jax.random.uniform(ks[6], (D_INNER,), jnp.float32, -4.0, -2.0), 'A_log': jnp.log(jnp.broadcast_to(jnp.arange(1, D_STATE + 1, dtype=jnp.float32), (D_INNER, D_STATE))), 'D': jnp.ones((D_INNER,), jnp.float32), 'W_out': jax.random.normal(ks[7], (D_MODEL, D_INNER), jnp.float32) * s(D_INNER), 'W_fc2': jax.random.normal(ks[8], (D_OUTPUT, D_MODEL), jnp.float32) * s(D_MODEL), 'b_fc2': jnp.zeros((D_OUTPUT,), jnp.float32)}
        return inp
    _L0_ffn_all = _L0_ffn_setup()
    _L0_ffn_in = {k: v for k, v in _L0_ffn_all.items() if k in ('W_fc1', 'b_fc1', 'W_in', 'conv_w', 'conv_b', 'W_xproj', 'W_dt', 'b_dt', 'A_log', 'D', 'W_out', 'W_fc2', 'b_fc2')}
    del _L0_ffn_all
    return {'x': x, 'adj': adj, 'L0_gnn_W': _L0_gnn_in['W'], 'L0_ffn_W_fc1': _L0_ffn_in['W_fc1'], 'L0_ffn_b_fc1': _L0_ffn_in['b_fc1'], 'L0_ffn_W_in': _L0_ffn_in['W_in'], 'L0_ffn_conv_w': _L0_ffn_in['conv_w'], 'L0_ffn_conv_b': _L0_ffn_in['conv_b'], 'L0_ffn_W_xproj': _L0_ffn_in['W_xproj'], 'L0_ffn_W_dt': _L0_ffn_in['W_dt'], 'L0_ffn_b_dt': _L0_ffn_in['b_dt'], 'L0_ffn_A_log': _L0_ffn_in['A_log'], 'L0_ffn_D': _L0_ffn_in['D'], 'L0_ffn_W_out': _L0_ffn_in['W_out'], 'L0_ffn_W_fc2': _L0_ffn_in['W_fc2'], 'L0_ffn_b_fc2': _L0_ffn_in['b_fc2']}

def reference(x, adj, L0_gnn_W, L0_ffn_W_fc1, L0_ffn_b_fc1, L0_ffn_W_in, L0_ffn_conv_w, L0_ffn_conv_b, L0_ffn_W_xproj, L0_ffn_W_dt, L0_ffn_b_dt, L0_ffn_A_log, L0_ffn_D, L0_ffn_W_out, L0_ffn_W_fc2, L0_ffn_b_fc2):
    import jax
    import jax.numpy as jnp

    def _L0_gnn_ref(input, A, W):
        import jax, jax.numpy as jnp
        import numpy as np
        N = 4096
        D = 256
        hidden = input * W
        return A @ hidden

    def _L0_ffn_ref(x, W_fc1, b_fc1, W_in, conv_w, conv_b, W_xproj, W_dt, b_dt, A_log, D, W_out, W_fc2, b_fc2):
        import jax, jax.numpy as jnp
        import numpy as np
        D_MODEL, D_STATE, D_CONV, D_INPUT, D_OUTPUT = (512, 16, 4, 256, 256)
        EXPAND = 2
        D_INNER = EXPAND * D_MODEL
        DT_RANK = (D_MODEL + 15) // 16
        B, L = (4, 1024)

        def _mamba(x, W_in, conv_w, conv_b, W_xproj, W_dt, b_dt, A_log, Dp, W_out):
            xz = jnp.einsum('bld,ed->ble', x, W_in)
            u, z = jnp.split(xz, 2, axis=-1)
            u_pad = jnp.pad(u, ((0, 0), (D_CONV - 1, 0), (0, 0)))
            u = sum((u_pad[:, k:k + u.shape[1], :] * conv_w[:, k] for k in range(D_CONV))) + conv_b
            u = jax.nn.silu(u)
            dbc = jnp.einsum('bld,ed->ble', u, W_xproj)
            dt, B_ssm, C_ssm = jnp.split(dbc, [DT_RANK, DT_RANK + D_STATE], axis=-1)
            delta = jax.nn.softplus(jnp.einsum('blr,dr->bld', dt, W_dt) + b_dt)
            A = -jnp.exp(A_log)

            def step(h, ins):
                d_t, B_t, C_t, u_t = ins
                dA = jnp.exp(d_t[..., None] * A)
                h = dA * h + (d_t * u_t)[..., None] * B_t[:, None, :]
                y_t = jnp.einsum('bds,bs->bd', h, C_t)
                return (h, y_t)
            h0 = jnp.zeros((u.shape[0], D_INNER, D_STATE), u.dtype)
            xs = (delta.transpose(1, 0, 2), B_ssm.transpose(1, 0, 2), C_ssm.transpose(1, 0, 2), u.transpose(1, 0, 2))
            _, y = jax.lax.scan(step, h0, xs)
            y = y.transpose(1, 0, 2) + u * Dp
            y = y * jax.nn.silu(z)
            return jnp.einsum('bld,ed->ble', y, W_out)
        h = jnp.einsum('bli,oi->blo', x, W_fc1) + b_fc1
        h = _mamba(h, W_in, conv_w, conv_b, W_xproj, W_dt, b_dt, A_log, D, W_out)
        return jnp.einsum('bld,od->blo', h, W_fc2) + b_fc2
    x = x + _L0_gnn_ref(_layernorm(x, axis=-1), adj, L0_gnn_W)
    x = x + _L0_ffn_ref(_layernorm(x, axis=-1)[None], L0_ffn_W_fc1, L0_ffn_b_fc1, L0_ffn_W_in, L0_ffn_conv_w, L0_ffn_conv_b, L0_ffn_W_xproj, L0_ffn_W_dt, L0_ffn_b_dt, L0_ffn_A_log, L0_ffn_D, L0_ffn_W_out, L0_ffn_W_fc2, L0_ffn_b_fc2)[0]
    return x

_drawn_inputs = setup_inputs


def setup_inputs(seed=0):
    import zlib

    import numpy as np

    out = dict(_drawn_inputs(seed))
    spreads = {'L0_gnn_W': (1.0, 0.2),
     'L0_ffn_b_fc1': (0.0, 0.287),
     'L0_ffn_conv_b': (0.0, 0.39),
     'L0_ffn_D': (1.0, 0.2),
     'L0_ffn_b_fc2': (0.0, 0.1)}
    factors = {'L0_ffn_b_dt': 11.826, 'L0_ffn_W_xproj': 2.752, 'L0_ffn_W_dt': 8.0, 'L0_ffn_A_log': 3.007}
    for name, (base, spread) in spreads.items():
        noise = np.random.default_rng([zlib.crc32(name.encode()), seed]).standard_normal(out[name].shape)
        drawn = base * np.exp(spread * noise) if base else spread * noise
        out[name] = jnp.asarray(drawn.astype(out[name].dtype))
    for name, factor in factors.items():
        out[name] = (out[name] * factor).astype(out[name].dtype)
    return out
```

```python
import concourse.bass as bass
from concourse import mybir
from contextlib import ExitStack

P = 128
N = 2048
D = 256
DM = 512
DI = 1024
NS = 16
R = 32
KC = 4
T = 512
NCH = N // T
NB = T // P
JB = N // P
G = DI // P
HG = G // 2
SLOTS = 2 * NS
CUT = 8
CLAMP = 30.0
SCLAMP = -40.0
EPS = 1e-5


def front_plan():
    quarters = [(i, q) for i in range(NB) for q in range(4)]
    order = [("z", g) for g in range(HG)]
    for a, (i, q) in enumerate(quarters):
        order.append(("T", i, q))
        if a:
            order.append(("M",) + quarters[a - 1])
        if a < HG:
            order.append(("z", HG + a))
    order.append(("M",) + quarters[-1])
    cost = {"T": 0.5, "M": 1.8, "z": 1.8, "u": 1.8, "xn": 0.3}
    plan = {s: [] for s in range(SLOTS)}
    s, used, waiting = CUT, 0.0, []
    zs = 0
    for piece in order:
        if used > 3.4:
            s, used = s + 1, 0.0
        while waiting and waiting[0][0] <= s and zs == G:
            plan[s].append(("xn", waiting.pop(0)[1]))
            used += cost["xn"]
        plan[s].append(piece)
        zs += piece[0] == "z"
        used += cost[piece[0]]
        if piece[0] == "M" and piece[2] == 3:
            waiting.append((s + 3, piece[1]))
    s = max(s + 1, waiting[-1][0])
    plan[s] += [("xn", i) for _, i in waiting]
    for g in range(G):
        plan[s + g // 2].append(("u", g))
    assert s + 3 <= SLOTS - 5, s
    plan[SLOTS - 2].append(("xp",))
    where = {p: s for s in plan for p in plan[s]}
    assert all(where[("M", i, 3)] < where[("M", i + 1, 0)] for i in range(NB - 1))
    return plan


def bank_of(job):
    kind = job[0]
    if kind in ("x1", "y", "xp", "ct"):
        return 0
    if kind in ("T", "z", "xn", "dt"):
        return 1
    return job[-1] % 2


def jobs_of(pieces):
    for p in pieces:
        if p[0] == "M":
            if p[2] == 0:
                yield ("x1", p[1])
        else:
            yield p


def numbered(jobs):
    count, out = [0, 0], {}
    for j in jobs:
        b = bank_of(j)
        assert j not in out
        out[j] = (b, count[b])
        count[b] += 1
    return out, count


def build(nc, x, adj, gnnW, W_fc1, b_fc1, W_in, conv_w, conv_b, W_xp, W_dt, b_dt, A_log, Dp, W_out, W_fc2,
          b_fc2, out):
    f32 = mybir.dt.float32
    ALU = mybir.AluOpType
    ACT = mybir.ActivationFunctionType

    PLAN = front_plan()
    FRONT = [p for s in range(SLOTS) for p in PLAN[s]]
    FRONT0 = [p for p in FRONT if p[0] != "z"]
    Z_LAST = [p for p in FRONT if p[0] == "z"]
    WEIGHTS = ([("wi", a) for a in range(16)] + [("wf", a) for a in range(2)] + [("wx", 0)]
               + [("wd", a) for a in range(2)] + [("wc", a) for a in range(8)] + [("bc", 0)]
               + [("wo", a) for a in range(4)])
    DT = [j for g in range(G) for j in (("dt", g), ("y", g))]
    UD = [("uD", j) for j in range(2 * NB)]
    OUTJ = [("o", b) for b in range(NB)]
    PRO, PRO_N = numbered(WEIGHTS + list(jobs_of(FRONT0)) + [("dt", g) for g in range(G)] + [("ct", 0)] + UD)
    LOOP, LOOP_N = numbered(list(jobs_of(FRONT)) + DT + [("ct", 0)] + UD + OUTJ)
    EPI, _ = numbered(Z_LAST + [("y", g) for g in range(G)] + OUTJ)

    def part(k):
        if k is None:
            return lambda job: (PRO[job][0], PRO[job][1])
        jobs = EPI if isinstance(k, int) and k == NCH - 1 else LOOP

        def at(job):
            b, n = jobs[job]
            return b, k * LOOP_N[b] + (PRO_N[b] + n)
        return at

    def wait(eng, sem, value):
        if isinstance(value, int) and value <= 0:
            return
        eng.wait_ge(sem, value)

    ctx = ExitStack()
    with ctx:
        def sb(name, shape):
            return ctx.enter_context(nc.sbuf_tensor(name, shape, f32))

        def pb(name, shape):
            return ctx.enter_context(nc.psum_tensor(name, shape, f32))

        def sem(name):
            return ctx.enter_context(nc.semaphore(name))

        Bscr = nc.dram_tensor("B_rows", [NCH, NS, T], f32, kind="Internal").ap()

        ident = sb("ident", [P, P])
        eps = sb("eps", [P, 1])
        pad = sb("pad", [P, 1])
        hid = sb("hid", [P, JB, D])
        WcT = sb("WcT", [P, 2, 2 * DI])
        WocT = sb("WocT", [P, G, D])
        WxT = sb("WxT", [P, G, R + 2 * NS])
        WdtT = sb("WdtT", [R, DI])
        diagD = sb("diagD", [P, G, P])
        Aneg = sb("Aneg", [P, G, NS])
        cw = sb("cw", [P, G, KC])
        cb = sb("cb", [P, G])
        bdt = sb("bdt", [P, G])
        Dcol = sb("Dcol", [P, G])
        bc = sb("bc", [P, 2 * G])
        bf1 = sb("bf1", [P, 4])
        b2 = sb("b2", [P, D])
        adj_in = sb("adj_in", [P, 2, N // 2])
        adjT = sb("adjT", [P, 2, 4, P])
        x1new = sb("x1new", [P, NB, D])
        x1cur = sb("x1cur", [P, NB, D])
        outst = sb("outst", [P, NB, D])
        xn = sb("xn", [P, 2, D])
        stats = sb("stats", [P, 2, 6])
        mv = sb("mv", [P, JB, 2])
        rstd = sb("rstd", [P, JB])
        xnT = sb("xnT", [P, 2, T])
        upre = sb("upre", [P, 2, T + KC])
        tails = sb("tails", [P, G, KC - 1])
        tmp = sb("tmp", [P, 2, T])
        dbc = sb("dbc", [R + 2 * NS, T])
        Ct = sb("Ct", [P, NB, NS])
        state = sb("state", [P, NS, G])
        h = sb("h", [P, 2, HG, T])
        yT = sb("yT", [P, NB, DI])
        delta = sb("delta", [P, G, T])
        du = sb("du", [P, G, T])
        gate = sb("gate", [P, G, T])
        u = sb("u", [P, G, T])
        Bbc = sb("Bbc", [P, 4, T])
        dBu = sb("dBu", [P, 4, T])
        win = [h[:, :, :, :].rearrange("p a b t -> p (a b) t"),
               yT[:, :, :].rearrange("p b (c t) -> p (b c) t", t=DM)]
        winT = [delta[:, :, :].rearrange("p (m c) t -> p m (c t)", m=2),
                du[:, :, :].rearrange("p (m c) t -> p m (c t)", m=2)]
        wout = gate[:, :, :].rearrange("p (m c) t -> p m (c t)", m=4)
        wfc1 = u[:, 0:2, :].rearrange("p a (b t) -> p (a b) t", b=2)
        wfc2 = u[:, 2:4, :]
        wfc2T = u[:, 4:6, :].rearrange("p a (b t) -> p (a b) t", b=2)
        wdt = u[:, 6, 0:G * R].rearrange("p (g r) -> p g r", r=R)
        wxp = Bbc[0:R + 2 * NS, 0:2, :].rearrange("p a t -> p (a t)")
        Wbc = dBu[:, 0, 0:D]

        dA = [pb(f"dA{i}", [P, T]) for i in range(2)]
        hT = [pb(f"hT{i}", [P, T]) for i in range(4)]
        misc = [pb(f"misc{i}", [P, T]) for i in range(2)]

        misc_ready = [sem(f"misc{i}_ready") for i in range(2)]
        misc_free = [sem(f"misc{i}_free") for i in range(2)]
        ident_made = sem("ident_made")
        pad_set = sem("pad_set")
        eps_made = sem("eps_made")
        x_in = sem("x_in")
        w_in = sem("w_in")
        c_in = sem("c_in")
        hid_chain = sem("hid_chain")
        hid_made = sem("hid_made")
        aneg_made = sem("aneg_made")
        diag_made = sem("diag_made")
        adj_loaded = [sem(f"adj_loaded{i}") for i in range(2)]
        x_loaded = sem("x_loaded")
        ln_step = sem("ln_step")
        rstd_step = sem("rstd_step")
        xn_made = sem("xn_made")
        x1_made = sem("x1_made")
        x1_moved = sem("x1_moved")
        upre_ready = sem("upre_ready")
        tails_saved = sem("tails_saved")
        conv_step = sem("conv_step")
        clamped = sem("clamped")
        sig_step = sem("sig_step")
        sig_used = sem("sig_used")
        b_stored = sem("b_stored")
        b_loaded = [sem(f"b_loaded{i}") for i in range(4)]
        sp_clamped = sem("sp_clamped")
        sp_step = sem("sp_step")
        delta_ready = sem("delta_ready")
        du_ready = sem("du_ready")
        dA_ready = sem("dA_ready")
        dBu_ready = sem("dBu_ready")
        scan_done = sem("scan_done")
        state_saved = sem("state_saved")
        hT_ready = sem("hT_ready")
        stt_done = sem("stt_done")
        out_stored = sem("out_stored")

        SC = 4
        STC = 4

        block = ctx.enter_context(nc.Block())

        def z_item(k, g):
            return k * 16 + (8 + g)

        def u_item(c, g):
            return c * 16 + g

        @block.sync
        def _(sp):
            def adj_load(c, i, hf, at):
                if i:
                    b, n = at(("T", i - 1, 2 * hf + 1))
                    sp.wait_ge(misc_ready[b], n + 1)
                else:
                    wait(sp, x1_made, c * NB)
                rows = bass.ts(c * NB + i, P)
                sp.dma_start(adj_in[:, hf, :], adj[rows, hf * (N // 2):(hf + 1) * (N // 2)])\
                    .then_inc(adj_loaded[hf], 16)

            def b_load(c, n, k_before, n_before):
                if n_before is not None:
                    used = k_before * 128 + (n_before + 1) * G
                    if n == 0 and not isinstance(c, int):
                        used = sp.to_reg(used)
                if n == 0:
                    sp.wait_ge(b_stored, (c + 1) * 16)
                if n_before is not None:
                    sp.wait_ge(dBu_ready, used)
                sp.dma_start(Bbc[:, n % 4, :], Bscr[c, n, :].partition_broadcast(P) if isinstance(c, int)
                             else Bscr[bass.ds(c, 1), n, :].rearrange("a t -> (a t)").partition_broadcast(P))\
                    .then_inc(b_loaded[n % 4], 16)

            def x_load(c):
                wait(sp, x1_moved, c)
                sp.dma_start(x1new[:, :, :], x[bass.ts(c, T), :].rearrange("(b p) d -> p b d", p=P))\
                    .then_inc(x_loaded, 16)

            def b_store(c, at):
                b, n = at(("xp",))
                sp.wait_ge(misc_free[b], n + 1)
                dst = Bscr[c, :, :] if isinstance(c, int) else Bscr[bass.ds(c, 1), :, :].rearrange("a n t -> (a n) t")
                sp.dma_start(dst, dbc[R:R + NS, :]).then_inc(b_stored, 16)

            def slot_loads(k, s):
                if s % 2 == 0 and s // 2 + 4 < NS:
                    b_load(k, s // 2 + 4, k, s // 2)

            def front_loads(c, at, pieces):
                for p in pieces:
                    if p[0] == "T" and p[2] % 2 and p[1] + 1 < NB:
                        adj_load(c, p[1] + 1, p[2] // 2, at)

            sp.dma_start(hid[:, :, :], x.rearrange("(b p) d -> p b d", p=P)).then_inc(x_in, 16)
            for a in range(2):
                sp.dma_start(win[a], W_in[a * DI:(a + 1) * DI, :].rearrange("(b p) m -> p b m", p=P))\
                    .then_inc(w_in, 16)
            sp.dma_start(wfc1, W_fc1.rearrange("(b p) m -> p b m", p=P)).then_inc(w_in, 16)
            sp.dma_start(wfc2, W_fc2.rearrange("(b p) m -> p b m", p=P)).then_inc(w_in, 16)
            sp.dma_start(wxp, W_xp).then_inc(w_in, 16)
            sp.dma_start(wdt, W_dt.rearrange("(b p) m -> p b m", p=P)).then_inc(w_in, 16)
            sp.dma_start(wout, W_out.rearrange("(b p) m -> p b m", p=P)).then_inc(w_in, 16)
            adj_load(0, 0, 0, None)
            adj_load(0, 0, 1, None)
            x_load(0)
            pro = part(None)
            front_loads(0, pro, FRONT0)
            b_store(0, pro)
            for n in range(4):
                b_load(0, n, 0, None)

            def opening(c):
                for s in range(CUT):
                    slot_loads(c, s)

            opening(0)

            def store_out(k, at):
                bk, n = at(("o", NB - 1))
                sp.wait_ge(misc_free[bk], n + 1)
                sp.dma_start(out[bass.ts(k, T), :].rearrange("(b p) d -> p b d", p=P), outst[:, :, :])\
                    .then_inc(out_stored, 16)

            with sp.Fori(0, NCH - 1) as k:
                at = part(k)
                x_load(k + 1)
                adj_load(k + 1, 0, 0, at)
                adj_load(k + 1, 0, 1, at)
                for s in range(CUT, SLOTS):
                    slot_loads(k, s)
                    front_loads(k + 1, at, PLAN[s])
                b_store(k + 1, at)
                for n in range(4):
                    b_load(k + 1, n, k, NS - 4 + n)
                opening(k + 1)
                store_out(k, at)
            k = NCH - 1
            for s in range(CUT, SLOTS):
                slot_loads(k, s)
            store_out(k, part(k))
            sp.wait_ge(out_stored, NCH * 16)

        @block.gpsimd
        def _(pool):
            slow = nc.allow_non_contiguous_dma(reason="one value per channel, once")
            ctx.enter_context(slow)
            pool.dma_start(Wbc, gnnW.partition_broadcast(P)).then_inc(c_in, 16)
            pool.dma_start(b2[:, :], b_fc2.partition_broadcast(P)).then_inc(c_in, 16)
            pool.dma_start(bf1[:, :], b_fc1.rearrange("(b p) -> p b", p=P)).then_inc(c_in, 16)
            pool.dma_start(cb[:, :], conv_b.rearrange("(b p) -> p b", p=P)).then_inc(c_in, 16)
            pool.dma_start(bdt[:, :], b_dt.rearrange("(b p) -> p b", p=P)).then_inc(c_in, 16)
            pool.dma_start(Dcol[:, :], Dp.rearrange("(b p) -> p b", p=P)).then_inc(c_in, 16)
            pool.dma_start(cw[:, :, :], conv_w.rearrange("(b p) m -> p b m", p=P)).then_inc(c_in, 16)
            pool.dma_start(Aneg[:, :, :], A_log.rearrange("(b p) m -> p b m", p=P)).then_inc(c_in, 16)
            nc.gpsimd.memset(eps[:, :], EPS).then_inc(eps_made, 1)
            nc.gpsimd.memset(ident[:, :], 0.0).then_inc(ident_made, 1)
            pool.wait_ge(ident_made, 1)
            nc.gpsimd.affine_select(out=ident[:, :], in_=ident[:, :], compare_op=ALU.not_equal, fill=1.0,
                                    base=0, pattern=[[-1, P]], channel_multiplier=1).then_inc(ident_made, 1)

            def sig_use(item, tensor, g):
                pool.wait_ge(sig_step, item * 3 + 3)
                nc.gpsimd.tensor_tensor(tensor[:, g, :], tensor[:, g, :], tmp[:, g % 2, :], ALU.mult)\
                    .then_inc(sig_used, 1)

            def du_make(c, g):
                pool.wait_ge(delta_ready, c * G + g + 1)
                pool.wait_ge(sig_used, u_item(c, g) + 1)
                nc.gpsimd.tensor_tensor(du[:, g, :], delta[:, g, :], u[:, g, :], ALU.mult).then_inc(du_ready, 1)

            def dBu_make(k, s, j):
                n, g = s // 2, (s % 2) * HG + j
                q = k * 128 + (s * 4 + j)
                if j == 0:
                    pool.wait_ge(b_loaded[n % 4], k * 64 + (n // 4 + 1) * 16)
                if s < 2:
                    pool.wait_ge(du_ready, k * G + g + 1)
                pool.wait_ge(scan_done, q + (SC - 3))
                nc.gpsimd.tensor_tensor(dBu[:, j, :], du[:, g, :], Bbc[:, n % 4, :], ALU.mult)\
                    .then_inc(dBu_ready, 1)

            def slot(k, s, items):
                for j in range(HG):
                    dBu_make(k, s, j)
                for f in items:
                    f()

            def front_items(k, c, s):
                for p in PLAN[s - 2]:
                    if p[0] == "z" and k is not None:
                        yield lambda g=p[1]: sig_use(z_item(k, g), gate, g)
                    if p[0] == "u" and c is not None:
                        yield lambda g=p[1]: sig_use(u_item(c, g), u, g)

            def opening(c):
                wait(pool, dBu_ready, c * 128)
                for g in range(G):
                    du_make(c, g)
                    dBu_make(c, g // HG, g % HG)
                for s in range(2, CUT):
                    slot(c, s, ())

            for g in range(G):
                sig_use(u_item(0, g), u, g)
            opening(0)
            with pool.Fori(0, NCH - 1) as k:
                for s in range(CUT, SLOTS):
                    slot(k, s, front_items(k, k + 1, s))
                opening(k + 1)
            for s in range(CUT, SLOTS):
                slot(NCH - 1, s, front_items(NCH - 1, None, s))

        @block.scalar
        def _(act):
            nc.scalar.preload_act_table_set("natural_log_exp_and_others")

            def read(at, job):
                b, n = at(job)
                act.wait_ge(misc_ready[b], n + 1)
                return misc[b], misc_free[b]

            def w_evac(at, job, dst, view=None, rows=P, cols=T):
                ps, free = read(at, job)
                src = ps[0:rows, 0:cols] if view is None else view(ps)
                nc.scalar.activation(dst, src, ACT.Copy).then_inc(free, 1)

            def dA_make(k, s, j):
                n, g = s // 2, (s % 2) * HG + j
                q = k * 128 + (s * 4 + j)
                if s < 2:
                    act.wait_ge(delta_ready, k * G + g + 1)
                act.wait_ge(scan_done, q + (SC - 1))
                nc.scalar.activation(dA[j % 2][:, :], delta[:, g, :], ACT.Exp, scale=Aneg[:, g, n:n + 1])\
                    .then_inc(dA_ready, 1)

            def sigmoid(item, g):
                t = tmp[:, g % 2, :]
                act.wait_ge(clamped, item + 1)
                nc.scalar.activation(t, t, ACT.Exp, scale=-1.0).then_inc(sig_step, 1)
                yield
                act.wait_ge(sig_step, item * 3 + 1)
                nc.scalar.activation(t, t, ACT.Ln, bias=1.0).then_inc(sig_step, 1)
                yield
                act.wait_ge(sig_step, item * 3 + 2)
                nc.scalar.activation(t, t, ACT.Exp, scale=-1.0).then_inc(sig_step, 1)
                yield

            def evac(c, at, p):
                if p[0] == "T":
                    ps, free = read(at, p)
                    nc.scalar.activation(adjT[:, p[2] % 2, :, :].rearrange("p a b -> p (a b)"), ps[:, :],
                                         ACT.Copy).then_inc(free, 1)
                elif p[0] == "xn":
                    ps, free = read(at, p)
                    nc.scalar.activation(xnT[:, :, p[1] * P:(p[1] + 1) * P],
                                         ps[:, 0:2 * P].rearrange("p (a b) -> p a b", a=2),
                                         ACT.Copy).then_inc(free, 1)
                elif p[0] == "z":
                    ps, free = read(at, p)
                    nc.scalar.activation(gate[:, p[1], :], ps[:, :], ACT.Identity,
                                         bias=bc[:, G + p[1]:G + p[1] + 1]).then_inc(free, 1)
                elif p[0] == "u":
                    g = p[1]
                    item = c * G + g
                    wait(act, conv_step, (item - 2) * 4 + 4)
                    act.wait_ge(tails_saved, item + (G - 1))
                    nc.scalar.activation(upre[:, g % 2, 1:KC], tails[:, g, :], ACT.Copy).then_inc(upre_ready, 1)
                    ps, free = read(at, p)
                    nc.scalar.activation(upre[:, g % 2, KC:KC + T], ps[:, :], ACT.Identity,
                                         bias=bc[:, g:g + 1]).then_inc(free, 1)
                    b, n = at(p)
                    act.wait_ge(misc_free[b], n + 1)
                    act.wait_ge(upre_ready, item + 1)
                    nc.scalar.activation(tails[:, g, :], upre[:, g % 2, T + 1:T + KC], ACT.Copy)\
                        .then_inc(tails_saved, 1)
                elif p[0] == "xp":
                    ps, free = read(at, p)
                    wait(act, b_stored, c * 16)
                    nc.scalar.activation(dbc[:, :], ps[0:R + 2 * NS, :], ACT.Copy).then_inc(free, 1)
                yield

            def inv_sqrt(step0, dst, var):
                nc.scalar.activation(dst, var, ACT.Ln, bias=eps[:, :]).then_inc(rstd_step, 1)
                act.wait_ge(rstd_step, step0 + 1)
                nc.scalar.activation(dst, dst, ACT.Exp, scale=-0.5).then_inc(rstd_step, 1)

            def row_rstd(c, i):
                step0 = (c * NB + i) * 2
                act.wait_ge(ln_step, step0 + 2)
                inv_sqrt(step0 + 2, rstd[:, i % 2:i % 2 + 1], mv[:, i % 2, 1:2])

            def slot(k, s, steps):
                for j in range(HG):
                    dA_make(k, s, j)
                for _ in steps:
                    pass

            def steps_of(k, c, at, s):
                for p in PLAN[s]:
                    if p[0] == "z" or p[0] in ("T", "xn") and c is not None:
                        yield from evac(c, at, p)
                for p in PLAN[s - 1]:
                    if p[0] == "M" and p[2] == 3 and c is not None:
                        row_rstd(c, p[1])
                        yield
                for p in PLAN[s - 2]:
                    if p[0] == "z" and k is not None:
                        yield from sigmoid(z_item(k, p[1]), p[1])
                    if p[0] == "u" and c is not None:
                        yield from sigmoid(u_item(c, p[1]), p[1])
                for p in PLAN[s]:
                    if p[0] in ("u", "xp") and c is not None:
                        yield from evac(c, at, p)

            def softplus(c, g):
                act.wait_ge(sp_clamped, c * G + g + 1)
                t = tmp[:, g % 2, :]
                nc.scalar.activation(t, t, ACT.Exp).then_inc(sp_step, 1)
                act.wait_ge(sp_step, (c * G + g) * 2 + 1)
                nc.scalar.activation(t, t, ACT.Ln, bias=1.0).then_inc(sp_step, 1)

            def dt_in(at, g):
                ps, free = read(at, ("dt", g))
                nc.scalar.activation(delta[:, g, :], ps[:, :], ACT.Identity, bias=bdt[:, g:g + 1])\
                    .then_inc(free, 1)

            def y_init(at, j):
                ps, free = read(at, ("uD", j))
                nc.scalar.activation(yT[:, j % NB, (j // NB) * T:(j // NB + 1) * T], ps[:, :], ACT.Copy)\
                    .then_inc(free, 1)

            def opening(c, at):
                wait(act, dA_ready, c * 128)
                dt_in(at, 0)
                for g in range(G):
                    if g + 1 < G:
                        dt_in(at, g + 1)
                    softplus(c, g)
                    if g >= 1 and g - 1 < 2:
                        dA_make(c, 0, g - 1)
                order = [("e", q) for q in range(2, G)]
                for j in range(2 * NB):
                    y_init(at, j)
                    if order:
                        _, q = order.pop(0)
                        dA_make(c, q // HG, q % HG)
                for s in range(2, CUT):
                    slot(c, s, iter(()))

            act.wait_ge(c_in, 8 * 16)
            act.wait_ge(eps_made, 1)
            nc.scalar.activation(Aneg[:, :, :], Aneg[:, :, :], ACT.Exp).then_inc(aneg_made, 1)
            act.wait_ge(aneg_made, 1)
            nc.scalar.activation(Aneg[:, :, :], Aneg[:, :, :], ACT.Copy, scale=-1.0).then_inc(aneg_made, 1)
            pro = part(None)
            for a in range(16):
                mb, eb = a // 4, a % 4
                w_evac(pro, ("wi", a), winT[mb // 2][:, mb % 2, eb * T:(eb + 1) * T])
            for a in range(2):
                w_evac(pro, ("wf", a), wfc2T[:, 2 * a:2 * a + 2, :].rearrange("p a b -> p (a b)"))
            w_evac(pro, ("wx", 0), WxT[:, :, :].rearrange("p a b -> p (a b)"))
            for a in range(2):
                w_evac(pro, ("wd", a), WdtT[:, a * T:(a + 1) * T], rows=R)
            for a in range(8):
                w_evac(pro, ("wc", a), WcT[:, a // 4, (a % 4) * T:(a % 4 + 1) * T])
            w_evac(pro, ("bc", 0), bc[:, :], cols=2 * G)
            for a in range(4):
                w_evac(pro, ("wo", a), WocT[:, 2 * a:2 * a + 2, :].rearrange("p a b -> p (a b)"))
            act.wait_ge(hid_chain, 2 * JB)
            act.wait_ge(stt_done, STC)
            inv_sqrt(0, rstd[:, :], mv[:, :, 1])
            for p in FRONT0:
                if p[0] == "xp":
                    for g in range(G - 2, G):
                        for _ in sigmoid(u_item(0, g), g):
                            pass
                if p[0] == "M" and p[2] == 3:
                    row_rstd(0, p[1])
                for _ in evac(0, pro, p):
                    pass
                if p[0] == "u" and p[1] >= 2:
                    for _ in sigmoid(u_item(0, p[1] - 2), p[1] - 2):
                        pass
            act.wait_ge(aneg_made, 2)
            opening(0, pro)
            with act.Fori(0, NCH - 1) as k:
                at = part(k)
                for s in range(CUT, SLOTS):
                    slot(k, s, steps_of(k, k + 1, at, s))
                opening(k + 1, at)
            k = NCH - 1
            at = part(k)
            for s in range(CUT, SLOTS):
                slot(k, s, steps_of(k, None, at, s))

        @block.vector
        def _(dve):
            def read(at, job):
                b, n = at(job)
                dve.wait_ge(misc_ready[b], n + 1)
                return misc[b], misc_free[b], n + 1

            nc.vector.memset(state[:, :, :], 0.0).then_inc(state_saved, SLOTS)
            nc.vector.memset(tails[:, :, :], 0.0).then_inc(tails_saved, G)
            nc.vector.memset(mv[:, :, :], 0.0).then_inc(scan_done, SC)
            nc.vector.memset(rstd[:, :], 0.0).then_inc(stt_done, STC)
            dve.wait_ge(x_in, 16)
            dve.wait_ge(c_in, 8 * 16)
            dve.wait_ge(scan_done, SC)
            for b in range(JB):
                if b >= 2:
                    dve.wait_ge(hid_chain, 2 * (b - 1))
                nc.vector.bn_stats(stats[:, b % 2, :], hid[:, b, :]).then_inc(hid_chain, 1)
                dve.wait_ge(hid_chain, 2 * b + 1)
                nc.vector.bn_aggr(mv[:, b, :], stats[:, b % 2, :]).then_inc(hid_chain, 1)
            dve.wait_ge(rstd_step, 2)
            for b in range(JB):
                nc.vector.tensor_scalar(hid[:, b, :], hid[:, b, :], mv[:, b, 0:1], rstd[:, b:b + 1],
                                        ALU.subtract, ALU.mult).then_inc(hid_made, 1)
            for b in range(JB):
                dve.wait_ge(hid_made, b + 1)
                nc.vector.tensor_tensor(hid[:, b, :], hid[:, b, :], Wbc, ALU.mult).then_inc(hid_made, 1)
            dve.wait_ge(hid_made, 2 * JB)
            dve.wait_ge(ident_made, 2)
            for g in range(G):
                nc.vector.tensor_scalar(diagD[:, g, :], ident[:, :], Dcol[:, g:g + 1], None, ALU.mult)\
                    .then_inc(diag_made, 1)

            def row_stats(c, at, i):
                ps, free, n = read(at, ("x1", i))
                r = i % 2
                base = (c * NB + i) * 2
                xr = x1new[:, i, :]
                dve.wait_ge(x_loaded, (c + 1) * 16)
                nc.vector.tensor_tensor(xr, ps[:, 0:D], xr, ALU.add).then_inc(free, 1)
                dve.wait_ge(free, n)
                wait(dve, ln_step, base - 2)
                nc.vector.bn_stats(stats[:, r, :], xr).then_inc(ln_step, 1)
                wait(dve, xn_made, c * NB + (i - 1))
                wait(dve, pad_set, c * NB + i)
                dve.wait_ge(ln_step, base + 1)
                nc.vector.memset(pad[:, :], 0.0).then_inc(pad_set, 1)
                nc.vector.bn_aggr(mv[:, r, :], stats[:, r, :]).then_inc(ln_step, 1)

            def normalize(c, at, i):
                r = i % 2
                xr = x1new[:, i, :]
                dve.wait_ge(rstd_step, (c * NB + i) * 2 + 4)
                if i >= 2:
                    b, n = at(("xn", i - 2))
                    dve.wait_ge(misc_ready[b], n + 1)
                nc.vector.tensor_scalar(xn[:, r, :], xr, mv[:, r, 0:1], rstd[:, r:r + 1],
                                        ALU.subtract, ALU.mult).then_inc(xn_made, 1)
                dve.wait_ge(xn_made, c * NB + (i + 1))
                nc.vector.tensor_tensor(xr, xr, b2[:, :], ALU.add).then_inc(x1_made, 1)

            def clamp(item, tensor, g):
                wait(dve, sig_used, item - 1)
                nc.vector.tensor_scalar(tmp[:, g % 2, :], tensor[:, g, :], SCLAMP, None, ALU.max)\
                    .then_inc(clamped, 1)

            def conv(c, at, g):
                base = (c * G + g) * 4
                b, n = at(("u", g))
                dve.wait_ge(misc_free[b], n + 1)
                dve.wait_ge(upre_ready, c * G + g + 1)
                src = upre[:, g % 2, :]
                nc.vector.tensor_scalar(u[:, g, :], src[:, KC:KC + T], cw[:, g, KC - 1:KC], cb[:, g:g + 1],
                                        ALU.mult, ALU.add).then_inc(conv_step, 1)
                for t in range(KC - 1):
                    dve.wait_ge(conv_step, base + t + 1)
                    nc.vector.scalar_tensor_tensor(u[:, g, :], src[:, 1 + t:1 + t + T], cw[:, g, t:t + 1],
                                                   u[:, g, :], ALU.mult, ALU.add).then_inc(conv_step, 1)
                dve.wait_ge(conv_step, base + 4)
                clamp(u_item(c, g), u, g)

            def scan(k, s, j):
                n, g = s // 2, (s % 2) * HG + j
                q = k * 128 + (s * 4 + j)
                dve.wait_ge(dA_ready, q + 1)
                dve.wait_ge(dBu_ready, q + 1)
                if j == 0:
                    wait(dve, hT_ready, k * 128 + (s * 4 - 4))
                    dve.wait_ge(state_saved, k * SLOTS + (s + SLOTS - 1))
                nc.vector.tensor_tensor_scan(h[:, s % 2, j, :], dA[j % 2][:, :], dBu[:, j, :],
                                             state[:, n, g:g + 1], ALU.mult, ALU.add).then_inc(scan_done, 1)

            def save_state(k, s):
                dve.wait_ge(scan_done, k * 128 + (s * 4 + 4 + SC))
                half = s % 2
                nc.vector.tensor_copy(state[:, s // 2, half * HG:(half + 1) * HG], h[:, half, :, T - 1])\
                    .then_inc(state_saved, 1)

            def weigh(k, s, b, at):
                n, half = s // 2, s % 2
                dve.wait_ge(hT_ready, k * 128 + (s * 4 + b + 1))
                if s < 2:
                    bk, m = at(("uD", half * NB + b))
                    dve.wait_ge(misc_free[bk], m + 1)
                else:
                    dve.wait_ge(stt_done, k * 128 + ((s - 2) * 4 + b + 1 + STC))
                y = yT[:, b, half * T:(half + 1) * T]
                nc.vector.scalar_tensor_tensor(y, hT[b][:, :], Ct[:, b, n:n + 1], y, ALU.mult, ALU.add)\
                    .then_inc(stt_done, 1)

            def slot(k, s, at, items, early=()):
                for f in early:
                    f()
                for j in range(HG):
                    scan(k, s, j)
                if s:
                    save_state(k, s - 1)
                    for b in range(NB):
                        weigh(k, s - 1, b, at)
                for f in items:
                    f()

            def front_items(k, c, at, s):
                for p in PLAN[s - 1]:
                    if p[0] == "z":
                        def z(g=p[1]):
                            b, n = at(("z", g))
                            dve.wait_ge(misc_free[b], n + 1)
                            if g < 2:
                                dve.wait_ge(delta_ready, (k + 1) * G)
                            clamp(z_item(k, g), gate, g)
                        yield z
                    elif c is None:
                        continue
                    elif p[0] == "u":
                        yield lambda g=p[1]: conv(c, at, g)
                for p in PLAN[s - 2]:
                    if p[0] == "M" and p[2] == 3 and c is not None:
                        yield lambda i=p[1]: normalize(c, at, i)

            def front_early(c, at, s):
                for p in PLAN[s - 1]:
                    if p[0] == "M" and p[2] == 3:
                        yield lambda i=p[1]: row_stats(c, at, i)

            def close_scan(k, at_k):
                save_state(k, SLOTS - 1)
                for b in range(NB):
                    weigh(k, SLOTS - 1, b, at_k)

            def gate_y(k, at, g):
                ps, free, _ = read(at, ("y", g))
                dve.wait_ge(sig_used, z_item(k, g) + 1)
                nc.vector.tensor_tensor(gate[:, g, :], ps[:, :], gate[:, g, :], ALU.mult).then_inc(free, 1)

            def opening(k, c, at):
                def cut(g):
                    b, n = at(("dt", g))
                    dve.wait_ge(misc_free[b], n + 1)
                    if g < 2:
                        dve.wait_ge(sig_used, u_item(c, G))
                    nc.vector.tensor_scalar(tmp[:, g % 2, :], delta[:, g, :], CLAMP, None, ALU.min)\
                        .then_inc(sp_clamped, 1)

                def top(g):
                    dve.wait_ge(sp_step, (c * G + g) * 2 + 2)
                    nc.vector.tensor_tensor(delta[:, g, :], delta[:, g, :], tmp[:, g % 2, :], ALU.max)\
                        .then_inc(delta_ready, 1)

                cut(0)
                for g in range(G):
                    if k is not None:
                        gate_y(k, at, g)
                    if g + 1 < G:
                        if g + 1 >= 2:
                            dve.wait_ge(delta_ready, c * G + g)
                        cut(g + 1)
                    top(g)
                ps, free, _ = read(at, ("ct", 0))
                dve.wait_ge(stt_done, c * 128 + STC)
                nc.vector.tensor_copy(Ct[:, :, :], ps[:, 0:NB * (R + 2 * NS)]
                                      .rearrange("p (b r) -> p b r", b=NB)[:, :, R + NS:]).then_inc(free, 1)
                b, n = at(("ct", 0))
                dve.wait_ge(misc_free[b], n + 1)
                for s in range(CUT):
                    late = s >= 2 and s % 2 == 0 and k is not None
                    slot(c, s, at, [lambda b=s // 2 - 1: finish(k, at, b)] if late else ())
                if k is not None:
                    finish(k, at, NB - 1)

            def finish(k, at, b):
                if b == 0:
                    wait(dve, out_stored, k * 16)
                    dve.wait_ge(x1_moved, k + 1)
                ps, free, _ = read(at, ("o", b))
                nc.vector.tensor_tensor(outst[:, b, :], ps[:, 0:D], x1cur[:, b, :], ALU.add).then_inc(free, 1)

            def move_x1(c, at):
                dve.wait_ge(x1_made, (c + 1) * NB)
                if at is not None:
                    b, n = at(("o", NB - 1))
                    dve.wait_ge(misc_free[b], n + 1)
                nc.vector.tensor_copy(x1cur[:, :, :], x1new[:, :, :]).then_inc(x1_moved, 1)

            pro = part(None)
            for p in FRONT0:
                if p[0] == "u":
                    conv(0, pro, p[1])
                elif p[0] == "M" and p[2] == 3:
                    row_stats(0, pro, p[1])
                    normalize(0, pro, p[1])
            opening(None, 0, pro)
            move_x1(0, None)
            with dve.Fori(0, NCH - 1) as k:
                at = part(k)
                for s in range(CUT, SLOTS):
                    slot(k, s, at, front_items(k, k + 1, at, s), front_early(k + 1, at, s))
                close_scan(k, at)
                opening(k, k + 1, at)
                move_x1(k + 1, at)
            k = NCH - 1
            at = part(k)
            for s in range(CUT, SLOTS):
                slot(k, s, at, front_items(k, None, at, s))
            close_scan(k, at)
            for g in range(G):
                gate_y(k, at, g)
            for b in range(NB):
                finish(k, at, b)

        @block.tensor
        def _(pe):
            def bank(at, job):
                b, n = at(job)
                wait(pe, misc_free[b], n)
                return misc[b], misc_ready[b]

            def turn(dst, src):
                k_, m_ = src.shape[0], src.shape[1]
                return nc.tensor.transpose(dst, src, ident[0:k_, 0:k_])

            def piece(c, at, p):
                if p[0] == "T":
                    ps, ready = bank(at, p)
                    _, i, q = p
                    pe.wait_ge(adj_loaded[q // 2], (c * NB + i + 1) * 16)
                    for a in range(4):
                        col = (q % 2) * T + a * P
                        last = turn(ps[:, a * P:(a + 1) * P], adj_in[:, q // 2, col:col + P])
                    last.then_inc(ready, 1)
                elif p[0] == "M":
                    _, i, q = p
                    b, n = at(("x1", i))
                    if q == 0:
                        wait(pe, misc_free[b], n)
                    bt, nt = at(("T", i, q))
                    pe.wait_ge(misc_free[bt], nt + 1)
                    for a in range(4):
                        last = nc.tensor.matmul(misc[b][:, 0:D], adjT[:, q % 2, a, :], hid[:, q * 4 + a, :],
                                                start=(q == 0 and a == 0), stop=(q == 3 and a == 3))
                    if q == 3:
                        last.then_inc(misc_ready[b], 1)
                elif p[0] == "xn":
                    i = p[1]
                    ps, ready = bank(at, p)
                    pe.wait_ge(xn_made, c * NB + i + 1)
                    for a in range(2):
                        last = turn(ps[:, a * P:(a + 1) * P], xn[:, i % 2, a * P:(a + 1) * P])
                    last.then_inc(ready, 1)
                elif p[0] in ("z", "u"):
                    g = p[1]
                    ps, ready = bank(at, p)
                    if p[0] == "u" and g == 0:
                        b, n = at(("xn", NB - 1))
                        pe.wait_ge(misc_free[b], n + 1)
                    col = (DI if p[0] == "z" else 0) + g * P
                    for a in range(2):
                        last = nc.tensor.matmul(ps[:, :], WcT[:, a, col:col + P], xnT[:, a, :],
                                                start=(a == 0), stop=(a == 1))
                    last.then_inc(ready, 1)
                elif p[0] == "xp":
                    ps, ready = bank(at, p)
                    for g in range(G):
                        pe.wait_ge(sig_used, u_item(c, g) + 1)
                        last = nc.tensor.matmul(ps[0:R + 2 * NS, :], WxT[:, g, :], u[:, g, :],
                                                start=(g == 0), stop=(g == G - 1))
                    last.then_inc(ready, 1)

            def turn_h(k, s):
                half = s % 2
                pe.wait_ge(scan_done, k * 128 + (s * 4 + 4 + SC))
                for b in range(NB):
                    pe.wait_ge(stt_done, k * 128 + (s * 4 + b - 3 + STC))
                    for j in range(HG):
                        last = turn(hT[b][:, j * P:(j + 1) * P], h[:, half, j, b * P:(b + 1) * P])
                    last.then_inc(hT_ready, 1)

            def dt_job(at, g):
                ps, ready = bank(at, ("dt", g))
                nc.tensor.matmul(ps[:, :], WdtT[:, g * P:(g + 1) * P], dbc[0:R, :], start=True, stop=True)\
                    .then_inc(ready, 1)

            def y_job(at, g):
                ps, ready = bank(at, ("y", g))
                for b in range(NB):
                    last = turn(ps[:, b * P:(b + 1) * P], yT[:, b, g * P:(g + 1) * P])
                last.then_inc(ready, 1)

            def out_job(at, b):
                ps, ready = bank(at, ("o", b))
                for g in range(G):
                    last = nc.tensor.matmul(ps[:, 0:D], gate[:, g, b * P:(b + 1) * P], WocT[:, g, :],
                                            start=(g == 0), stop=(g == G - 1))
                last.then_inc(ready, 1)

            def boundary(k, c, at):
                b, n = at(("xp",))
                pe.wait_ge(misc_free[b], n + 1)
                dt_job(at, 0)
                if k is not None:
                    turn_h(k, SLOTS - 1)
                    pe.wait_ge(stt_done, k * 128 + (128 + STC))
                for g in range(G):
                    if k is not None:
                        y_job(at, g)
                    if g + 1 < G:
                        dt_job(at, g + 1)
                ps, ready = bank(at, ("ct", 0))
                w = R + 2 * NS
                for b in range(NB):
                    last = nc.tensor.matmul(ps[:, b * w:(b + 1) * w], dbc[:, b * P:(b + 1) * P],
                                            ident[0:w, 0:w], start=True, stop=True)
                last.then_inc(ready, 1)
                for j in range(2 * NB):
                    ps, ready = bank(at, ("uD", j))
                    b = j % NB
                    for a in range(HG):
                        g = (j // NB) * HG + a
                        last = nc.tensor.matmul(ps[:, a * P:(a + 1) * P], u[:, g, b * P:(b + 1) * P],
                                                diagD[:, g, :], start=True, stop=True)
                    last.then_inc(ready, 1)

            pro = part(None)
            pe.wait_ge(ident_made, 2)
            pe.wait_ge(w_in, 16 * 7)
            for a in range(16):
                ps, ready = bank(pro, ("wi", a))
                mb, eb = a // 4, a % 4
                for e in range(4):
                    row = eb * 4 + e
                    last = turn(ps[:, e * P:(e + 1) * P], win[row // 8][:, row % 8, mb * P:(mb + 1) * P])
                last.then_inc(ready, 1)
            for a in range(2):
                ps, ready = bank(pro, ("wf", a))
                for e in range(4):
                    mb, ob = 2 * a + e // 2, e % 2
                    last = turn(ps[:, e * P:(e + 1) * P], wfc2[:, ob, mb * P:(mb + 1) * P])
                last.then_inc(ready, 1)
            ps, ready = bank(pro, ("wx", 0))
            w = R + 2 * NS
            for g in range(G):
                last = turn(ps[:, g * w:(g + 1) * w], wxp[:, g * P:(g + 1) * P])
            last.then_inc(ready, 1)
            for a in range(2):
                ps, ready = bank(pro, ("wd", a))
                for e in range(4):
                    last = nc.tensor.matmul(ps[0:R, e * P:(e + 1) * P], wdt[:, a * 4 + e, :], ident[:, :],
                                            start=True, stop=True)
                last.then_inc(ready, 1)
            b, n = pro(("wi", 15))
            pe.wait_ge(misc_free[b], n + 1)
            b, n = pro(("wi", 14))
            pe.wait_ge(misc_free[b], n + 1)
            for a in range(8):
                ps, ready = bank(pro, ("wc", a))
                ib, eb = a // 4, a % 4
                for mb in range(4):
                    last = nc.tensor.matmul(ps[:, :], wfc1[:, mb, ib * P:(ib + 1) * P],
                                            winT[mb // 2][:, mb % 2, eb * T:(eb + 1) * T],
                                            start=(mb == 0), stop=(mb == 3))
                last.then_inc(ready, 1)
            ps, ready = bank(pro, ("bc", 0))
            pe.wait_ge(c_in, 8 * 16)
            for e in range(2 * G):
                for mb in range(4):
                    last = nc.tensor.matmul(ps[:, e:e + 1], winT[mb // 2][:, mb % 2, e * P:(e + 1) * P],
                                            bf1[:, mb:mb + 1], start=(mb == 0), stop=(mb == 3))
            last.then_inc(ready, 1)
            for a in range(4):
                ps, ready = bank(pro, ("wo", a))
                for e in range(2):
                    g = 2 * a + e
                    for mb in range(4):
                        last = nc.tensor.matmul(ps[:, e * D:(e + 1) * D], wout[:, mb, g * P:(g + 1) * P],
                                                wfc2T[:, mb, :], start=(mb == 0), stop=(mb == 3))
                last.then_inc(ready, 1)
            pe.wait_ge(hid_made, 2 * JB)
            for p in FRONT0:
                if p[0] == "u" and p[1] == 0:
                    for name in ("bc", "wc", "wo"):
                        b, n = pro((name, {"bc": 0, "wc": 7, "wo": 3}[name]))
                        pe.wait_ge(misc_free[b], n + 1)
                piece(0, pro, p)
            pe.wait_ge(diag_made, G)
            boundary(None, 0, pro)
            for s in range(1, CUT):
                turn_h(0, s - 1)
            with pe.Fori(0, NCH - 1) as k:
                at = part(k)
                for s in range(CUT, SLOTS):
                    turn_h(k, s - 1)
                    for p in PLAN[s]:
                        piece(k + 1, at, p)
                boundary(k, k + 1, at)
                for s in range(1, CUT):
                    turn_h(k + 1, s - 1)
                    if s % 2:
                        out_job(at, s // 2)
            k = NCH - 1
            at = part(k)
            for s in range(CUT, SLOTS):
                turn_h(k, s - 1)
                for p in PLAN[s]:
                    if p[0] == "z":
                        piece(None, at, p)
            turn_h(k, SLOTS - 1)
            pe.wait_ge(stt_done, k * 128 + 128 + STC)
            for g in range(G):
                y_job(at, g)
            b, n = at(("y", G - 1))
            pe.wait_ge(misc_free[b], n + 1)
            for b in range(NB):
                out_job(at, b)


_INS = ['x', 'adj', 'L0_gnn_W', 'L0_ffn_W_fc1', 'L0_ffn_b_fc1', 'L0_ffn_W_in', 'L0_ffn_conv_w', 'L0_ffn_conv_b',
        'L0_ffn_W_xproj', 'L0_ffn_W_dt', 'L0_ffn_b_dt', 'L0_ffn_A_log', 'L0_ffn_D', 'L0_ffn_W_out',
        'L0_ffn_W_fc2', 'L0_ffn_b_fc2']


def kernel(**inputs):
    import numpy as _np
    import concourse.bacc as _bacc
    from concourse import mybir as _mybir
    from concourse.bass_utils import run_bass_kernel_spmd as _run

    nc = _bacc.Bacc("TRN2", target_bir_lowering=False, num_devices=1)
    arrays, args = {}, []
    for name in _INS:
        a = _np.ascontiguousarray(inputs[name])
        arrays[f"in_{name}"] = a
        args.append(nc.dram_tensor(f"in_{name}", a.shape, _mybir.dt.from_np(a.dtype), kind="ExternalInput").ap())
    args.append(nc.dram_tensor("out_0", (N, D), _mybir.dt.float32, kind="ExternalOutput").ap())
    build(nc, *args)
    r = _run(nc, [arrays], core_ids=[0])
    return r.results[0]["out_0"]
```

```python
import concourse.bass as bass
from concourse import mybir
from contextlib import ExitStack

P = 128
N = 2048
D = 256
DM = 512
DI = 1024
NS = 16
R = 32
KC = 4
T = 512
NCH = N // T
NB = T // P
JB = N // P
G = DI // P
HG = G // 2
SLOTS = 2 * NS
CUT = 8
CLAMP = 30.0
SCLAMP = -40.0
EPS = 1e-5


def front_plan():
    quarters = [(i, q) for i in range(NB) for q in range(4)]
    plan = {s: [] for s in range(SLOTS)}
    slot_of = [CUT + 3 * (a // 4) + min(a % 4, 2) for a in range(4 * NB)]
    for a, (i, q) in enumerate(quarters):
        s = slot_of[a]
        plan[s].append(("T", i, q))
        if a:
            plan[s].append(("M",) + quarters[a - 1])
        if a % 4 < 2:
            plan[s].append(("z", a // 4 * 2 + a % 4))
    plan[20].append(("M",) + quarters[-1])
    where = {p: s for s in plan for p in plan[s]}
    assert all(where[("M", i, 3)] < where[("M", i + 1, 0)] for i in range(NB - 1))
    for i in range(NB):
        plan[max(where[("M", i, 3)] + 2, where[("z", G - 1)] + 1)].insert(0, ("xn", i))
    first = where[("M", NB - 1, 3)] + 2
    for g in range(G):
        plan[first + g // 2].append(("u", g))
    last = first + (G - 1) // 2
    plan[last + 4].append(("xp",))
    plan[last + 5] += [("dt", g) for g in range(HG)]
    plan[last + 6] += [("dt", g) for g in range(HG, HG + 2)]
    assert last + 6 == SLOTS - 1
    return plan


def bank_of(job):
    kind = job[0]
    if kind in ("x1", "xp", "ct"):
        return 0
    if kind in ("T", "z", "xn"):
        return 1
    return job[-1] % 2


def jobs_of(pieces):
    for p in pieces:
        if p[0] == "M":
            if p[2] == 0:
                yield ("x1", p[1])
        else:
            yield p


def numbered(jobs):
    count, out = [0, 0], {}
    for j in jobs:
        b = bank_of(j)
        assert j not in out
        out[j] = (b, count[b])
        count[b] += 1
    return out, count


def build(nc, x, adj, gnnW, W_fc1, b_fc1, W_in, conv_w, conv_b, W_xp, W_dt, b_dt, A_log, Dp, W_out, W_fc2,
          b_fc2, out):
    f32 = mybir.dt.float32
    ALU = mybir.AluOpType
    ACT = mybir.ActivationFunctionType

    PLAN = front_plan()
    FRONT = [p for s in range(SLOTS) for p in PLAN[s]]
    FRONT0 = [p for p in FRONT if p[0] != "z"]
    Z_LAST = [p for p in FRONT if p[0] == "z"]
    WEIGHTS = ([("wi", a) for a in range(16)] + [("wf", a) for a in range(2)] + [("wx", 0)]
               + [("wd", a) for a in range(2)] + [("wc", a) for a in range(8)] + [("bc", 0)])
    DT = [("dt", g) for g in range(HG + 2, G)]
    Y = [("y", g) for g in range(G)]
    UD = [("uD", j) for j in range(2 * NB)]
    OUTJ = [("o", b) for b in range(NB)]
    PRO, PRO_N = numbered(WEIGHTS + list(jobs_of(FRONT0)) + DT + [("ct", 0)] + UD + [("wo", a) for a in range(4)])
    LOOP, LOOP_N = numbered(list(jobs_of(FRONT)) + DT + [("ct", 0)] + Y + UD + OUTJ)
    EPI, _ = numbered(Z_LAST + Y + OUTJ)

    def part(k):
        if k is None:
            return lambda job: (PRO[job][0], PRO[job][1])
        jobs = EPI if isinstance(k, int) and k == NCH - 1 else LOOP

        def at(job):
            b, n = jobs[job]
            return b, k * LOOP_N[b] + (PRO_N[b] + n)
        return at

    def wait(eng, sem, value):
        if isinstance(value, int) and value <= 0:
            return
        eng.wait_ge(sem, value)

    ctx = ExitStack()
    with ctx:
        def sb(name, shape):
            return ctx.enter_context(nc.sbuf_tensor(name, shape, f32))

        def pb(name, shape):
            return ctx.enter_context(nc.psum_tensor(name, shape, f32))

        def sem(name):
            return ctx.enter_context(nc.semaphore(name))

        Bscr = nc.dram_tensor("B_rows", [NCH, NS, T], f32, kind="Internal").ap()

        ident = sb("ident", [P, P])
        eps = sb("eps", [P, 1])
        pad = sb("pad", [P, 1])
        hid = sb("hid", [P, JB, D])
        WcT = sb("WcT", [P, 2, 2 * DI])
        WocT = sb("WocT", [P, G, D])
        WxT = sb("WxT", [P, G, R + 2 * NS])
        WdtT = sb("WdtT", [R, DI])
        diagD = sb("diagD", [P, G, P])
        Aneg = sb("Aneg", [P, G, NS])
        cw = sb("cw", [P, G, KC])
        cb = sb("cb", [P, G])
        bdt = sb("bdt", [P, G])
        Dcol = sb("Dcol", [P, G])
        bc = sb("bc", [P, 2 * G])
        bf1 = sb("bf1", [P, 4])
        b2 = sb("b2", [P, D])
        adj_in = sb("adj_in", [P, 2, N // 2])
        adjT = sb("adjT", [P, 2, 4, P])
        x1new = sb("x1new", [P, NB, D])
        x1cur = sb("x1cur", [P, NB, D])
        stats = sb("stats", [P, 2, 6])
        mv = sb("mv", [P, JB, 2])
        rstd = sb("rstd", [P, JB])
        xnT = sb("xnT", [P, 2, T])
        upre = sb("upre", [P, 2, T + KC])
        tails = sb("tails", [P, G, KC - 1])
        tmp = sb("tmp", [P, 4, T])
        dbc = sb("dbc", [R + 2 * NS, T])
        Ct = sb("Ct", [P, NB, NS])
        state = sb("state", [P, NS, G])
        h = sb("h", [P, 2, HG, T])
        yT = sb("yT", [P, NB, DI])
        delta = sb("delta", [P, G, T])
        du = sb("du", [P, G, T])
        gate = sb("gate", [P, G, T])
        u = sb("u", [P, G, T])
        Bbc = sb("Bbc", [P, 4, T])
        dBu = sb("dBu", [P, 4, T])
        xn = [upre[:, i % 2, KC + i // 2 * D:KC + (i // 2 + 1) * D] for i in range(NB)]
        vdt = adj_in[:, :, :].rearrange("p a (b t) -> p (a b) t", t=T)
        win = [h[:, :, :, :].rearrange("p a b t -> p (a b) t"),
               yT[:, :, :].rearrange("p b (c t) -> p (b c) t", t=DM)]
        winT = [delta[:, :, :].rearrange("p (m c) t -> p m (c t)", m=2),
                du[:, :, :].rearrange("p (m c) t -> p m (c t)", m=2)]
        wout = gate[:, :, :].rearrange("p (m c) t -> p m (c t)", m=4)
        wfc1 = u[:, 0:2, :].rearrange("p a (b t) -> p (a b) t", b=2)
        wfc2 = u[:, 2:4, :]
        wfc2T = x1cur
        wdt = u[:, 6, 0:G * R].rearrange("p (g r) -> p g r", r=R)
        wxp = Bbc[0:R + 2 * NS, 0:2, :].rearrange("p a t -> p (a t)")
        Wbc = dBu[:, 0, 0:D]

        dA = [pb(f"dA{i}", [P, T]) for i in range(2)]
        hT = [pb(f"hT{i}", [P, T]) for i in range(4)]
        misc = [pb(f"misc{i}", [P, T]) for i in range(2)]

        misc_ready = [sem(f"misc{i}_ready") for i in range(2)]
        misc_free = [sem(f"misc{i}_free") for i in range(2)]
        ident_made = sem("ident_made")
        pad_set = sem("pad_set")
        eps_made = sem("eps_made")
        x_in = sem("x_in")
        w_first = sem("w_first")
        w_in = sem("w_in")
        w_out = sem("w_out")
        c_in = sem("c_in")
        hid_chain = sem("hid_chain")
        hid_made = sem("hid_made")
        aneg_made = sem("aneg_made")
        diag_made = sem("diag_made")
        adj_loaded = [sem(f"adj_loaded{i}") for i in range(2)]
        x_loaded = sem("x_loaded")
        ln_step = sem("ln_step")
        rstd_step = sem("rstd_step")
        xn_made = sem("xn_made")
        x1_made = sem("x1_made")
        x1_moved = sem("x1_moved")
        upre_ready = sem("upre_ready")
        tails_saved = sem("tails_saved")
        conv_step = sem("conv_step")
        clamped = sem("clamped")
        sig_step = sem("sig_step")
        sig_used = sem("sig_used")
        b_stored = sem("b_stored")
        b_loaded = [sem(f"b_loaded{i}") for i in range(4)]
        sp_clamped = sem("sp_clamped")
        sp_step = sem("sp_step")
        delta_ready = sem("delta_ready")
        du_ready = sem("du_ready")
        dA_ready = sem("dA_ready")
        dBu_ready = sem("dBu_ready")
        scan_done = sem("scan_done")
        state_saved = sem("state_saved")
        hT_ready = sem("hT_ready")
        stt_done = sem("stt_done")
        out_stored = sem("out_stored")

        SC = 4
        STC = 4

        block = ctx.enter_context(nc.Block())

        def z_item(k, g):
            return k * 16 + (8 + g)

        def u_item(c, g):
            return c * 16 + g

        @block.sync
        def _(sp):
            def adj_load(c, i, hf, at):
                if i:
                    b, n = at(("T", i - 1, 2 * hf + 1))
                    sp.wait_ge(misc_ready[b], n + 1)
                else:
                    wait(sp, delta_ready, c * G - HG)
                rows = bass.ts(c * NB + i, P)
                sp.dma_start(adj_in[:, hf, :], adj[rows, hf * (N // 2):(hf + 1) * (N // 2)])\
                    .then_inc(adj_loaded[hf], 16)

            def b_load(c, n, k_before, n_before):
                if n_before is not None:
                    used = k_before * 128 + (n_before + 1) * G
                    if n == 0 and not isinstance(c, int):
                        used = sp.to_reg(used)
                if n == 0:
                    sp.wait_ge(b_stored, (c + 1) * 16)
                if n_before is not None:
                    sp.wait_ge(dBu_ready, used)
                sp.dma_start(Bbc[:, n % 4, :], Bscr[c, n, :].partition_broadcast(P) if isinstance(c, int)
                             else Bscr[bass.ds(c, 1), n, :].rearrange("a t -> (a t)").partition_broadcast(P))\
                    .then_inc(b_loaded[n % 4], 16)

            def x_load(c):
                wait(sp, x1_moved, c)
                sp.dma_start(x1new[:, :, :], x[bass.ts(c, T), :].rearrange("(b p) d -> p b d", p=P))\
                    .then_inc(x_loaded, 16)

            def b_store(c, at):
                b, n = at(("xp",))
                sp.wait_ge(misc_free[b], n + 1)
                dst = Bscr[c, :, :] if isinstance(c, int) else Bscr[bass.ds(c, 1), :, :].rearrange("a n t -> (a n) t")
                sp.dma_start(dst, dbc[R:R + NS, :]).then_inc(b_stored, 16)

            def slot_loads(k, s):
                if s % 2 == 0 and 0 < s and s // 2 + 3 < NS:
                    b_load(k, s // 2 + 3, k, s // 2 - 1)

            def front_loads(c, at, pieces):
                for p in pieces:
                    if p[0] == "T" and p[2] % 2 and p[1] + 1 < NB:
                        adj_load(c, p[1] + 1, p[2] // 2, at)

            def w_load(dst, src, done):
                sp.dma_start(dst, src).then_inc(done, 16)

            def blocks(w):
                return w.rearrange("(b p) m -> p b m", p=P)

            w_load(win[0], blocks(W_in[0:DI, :]), w_first)
            w_load(wfc2, blocks(W_fc2), w_in)
            w_load(win[1], blocks(W_in[DI:2 * DI, :]), w_in)
            w_load(wxp, W_xp, w_in)
            w_load(wdt, blocks(W_dt), w_in)
            w_load(wfc1, blocks(W_fc1), w_in)
            w_load(hid[:, :, :], blocks(x), x_in)
            adj_load(0, 0, 0, None)
            adj_load(0, 0, 1, None)
            x_load(0)
            w_load(wout, blocks(W_out), w_out)
            pro = part(None)
            front_loads(0, pro, FRONT0)
            b_store(0, pro)
            for n in range(4):
                b_load(0, n, 0, None)

            def opening(c):
                for s in range(CUT):
                    slot_loads(c, s)

            opening(0)

            def store_out(k, at):
                bk, n = at(("o", NB - 1))
                sp.wait_ge(misc_free[bk], n + 1)
                sp.dma_start(out[bass.ts(k, T), :].rearrange("(b p) d -> p b d", p=P), x1cur[:, :, :])\
                    .then_inc(out_stored, 16)

            with sp.Fori(0, NCH - 1) as k:
                at = part(k)
                adj_load(k + 1, 0, 0, at)
                adj_load(k + 1, 0, 1, at)
                for s in range(CUT, SLOTS):
                    if s == CUT + 2:
                        x_load(k + 1)
                    slot_loads(k, s)
                    front_loads(k + 1, at, PLAN[s])
                b_store(k + 1, at)
                for n in range(4):
                    b_load(k + 1, n, k, NS - 4 + n)
                opening(k + 1)
                store_out(k, at)
            k = NCH - 1
            for s in range(CUT, SLOTS):
                slot_loads(k, s)
            store_out(k, part(k))
            sp.wait_ge(out_stored, NCH * 16)

        @block.gpsimd
        def _(pool):
            slow = nc.allow_non_contiguous_dma(reason="one value per channel, once")
            ctx.enter_context(slow)
            pool.dma_start(Wbc, gnnW.partition_broadcast(P)).then_inc(c_in, 16)
            pool.dma_start(b2[:, :], b_fc2.partition_broadcast(P)).then_inc(c_in, 16)
            pool.dma_start(bf1[:, :], b_fc1.rearrange("(b p) -> p b", p=P)).then_inc(c_in, 16)
            pool.dma_start(cb[:, :], conv_b.rearrange("(b p) -> p b", p=P)).then_inc(c_in, 16)
            pool.dma_start(bdt[:, :], b_dt.rearrange("(b p) -> p b", p=P)).then_inc(c_in, 16)
            pool.dma_start(Dcol[:, :], Dp.rearrange("(b p) -> p b", p=P)).then_inc(c_in, 16)
            pool.dma_start(cw[:, :, :], conv_w.rearrange("(b p) m -> p b m", p=P)).then_inc(c_in, 16)
            pool.dma_start(Aneg[:, :, :], A_log.rearrange("(b p) m -> p b m", p=P)).then_inc(c_in, 16)
            nc.gpsimd.memset(eps[:, :], EPS).then_inc(eps_made, 1)
            nc.gpsimd.memset(ident[:, :], 0.0).then_inc(ident_made, 1)
            pool.wait_ge(ident_made, 1)
            nc.gpsimd.affine_select(out=ident[:, :], in_=ident[:, :], compare_op=ALU.not_equal, fill=1.0,
                                    base=0, pattern=[[-1, P]], channel_multiplier=1).then_inc(ident_made, 1)

            def sig_use(item, tensor, g):
                pool.wait_ge(sig_step, item * 3 + 3)
                nc.gpsimd.tensor_tensor(tensor[:, g, :], tensor[:, g, :], tmp[:, g % 4, :], ALU.mult)\
                    .then_inc(sig_used, 1)

            def du_make(c, g):
                pool.wait_ge(delta_ready, c * G + g + 1)
                pool.wait_ge(sig_used, u_item(c, g) + 1)
                nc.gpsimd.tensor_tensor(du[:, g, :], delta[:, g, :], u[:, g, :], ALU.mult).then_inc(du_ready, 1)

            def dBu_make(k, s, j):
                n, g = s // 2, (s % 2) * HG + j
                q = k * 128 + (s * 4 + j)
                if j == 0:
                    pool.wait_ge(b_loaded[n % 4], k * 64 + (n // 4 + 1) * 16)
                if s < 2:
                    pool.wait_ge(du_ready, k * G + g + 1)
                pool.wait_ge(scan_done, q + (SC - 3))
                nc.gpsimd.tensor_tensor(dBu[:, j, :], du[:, g, :], Bbc[:, n % 4, :], ALU.mult)\
                    .then_inc(dBu_ready, 1)

            def slot(k, s, items):
                items = list(items)
                for j in range(HG):
                    dBu_make(k, s, j)
                    if j % 2 and items:
                        items.pop(0)()

            def front_items(k, c, s):
                for p in PLAN[s - 4]:
                    if p[0] == "z":
                        yield lambda g=p[1]: sig_use(z_item(k, g), gate, g)
                for p in PLAN[s - 3]:
                    if p[0] == "u" and c is not None:
                        yield lambda g=p[1]: sig_use(u_item(c, g), u, g)

            def opening(c):
                wait(pool, dBu_ready, c * 128)
                for g in range(G):
                    du_make(c, g)
                    dBu_make(c, g // HG, g % HG)
                for s in range(2, CUT):
                    slot(c, s, ())

            for g in range(G):
                sig_use(u_item(0, g), u, g)
            opening(0)
            with pool.Fori(0, NCH - 1) as k:
                for s in range(CUT, SLOTS):
                    slot(k, s, front_items(k, k + 1, s))
                opening(k + 1)
            for s in range(CUT, SLOTS):
                slot(NCH - 1, s, front_items(NCH - 1, None, s))

        @block.scalar
        def _(act):
            nc.scalar.preload_act_table_set("natural_log_exp_and_others")

            def read(at, job):
                b, n = at(job)
                act.wait_ge(misc_ready[b], n + 1)
                return misc[b], misc_free[b]

            def w_evac(at, job, dst, view=None, rows=P, cols=T):
                ps, free = read(at, job)
                src = ps[0:rows, 0:cols] if view is None else view(ps)
                nc.scalar.activation(dst, src, ACT.Copy).then_inc(free, 1)

            def dA_make(k, s, j):
                n, g = s // 2, (s % 2) * HG + j
                q = k * 128 + (s * 4 + j)
                if s < 2:
                    act.wait_ge(delta_ready, k * G + g + 1)
                act.wait_ge(scan_done, q + (SC - 1))
                nc.scalar.activation(dA[j % 2][:, :], delta[:, g, :], ACT.Exp, scale=Aneg[:, g, n:n + 1])\
                    .then_inc(dA_ready, 1)

            def sigmoid(item, tensor, g):
                t = tmp[:, g % 4, :]
                act.wait_ge(clamped, item + 1)
                wait(act, sig_used, item - 3)
                nc.scalar.activation(t, tensor[:, g, :], ACT.Exp, scale=-1.0).then_inc(sig_step, 1)
                yield
                act.wait_ge(sig_step, item * 3 + 1)
                nc.scalar.activation(t, t, ACT.Ln, bias=1.0).then_inc(sig_step, 1)
                yield
                act.wait_ge(sig_step, item * 3 + 2)
                nc.scalar.activation(t, t, ACT.Exp, scale=-1.0).then_inc(sig_step, 1)
                yield

            def evac(c, at, p):
                if p[0] == "T":
                    ps, free = read(at, p)
                    nc.scalar.activation(adjT[:, p[2] % 2, :, :].rearrange("p a b -> p (a b)"), ps[:, :],
                                         ACT.Copy).then_inc(free, 1)
                elif p[0] == "xn":
                    ps, free = read(at, p)
                    nc.scalar.activation(xnT[:, :, p[1] * P:(p[1] + 1) * P],
                                         ps[:, 0:2 * P].rearrange("p (a b) -> p a b", a=2),
                                         ACT.Copy).then_inc(free, 1)
                elif p[0] == "z":
                    ps, free = read(at, p)
                    nc.scalar.activation(gate[:, p[1], :], ps[:, :], ACT.Identity,
                                         bias=bc[:, G + p[1]:G + p[1] + 1]).then_inc(free, 1)
                elif p[0] == "u":
                    g = p[1]
                    item = c * G + g
                    wait(act, conv_step, (item - 2) * 4 + 4)
                    act.wait_ge(tails_saved, item + (G - 1))
                    nc.scalar.activation(upre[:, g % 2, 1:KC], tails[:, g, :], ACT.Copy).then_inc(upre_ready, 1)
                    ps, free = read(at, p)
                    nc.scalar.activation(upre[:, g % 2, KC:KC + T], ps[:, :], ACT.Identity,
                                         bias=bc[:, g:g + 1]).then_inc(free, 1)
                    b, n = at(p)
                    act.wait_ge(misc_free[b], n + 1)
                    act.wait_ge(upre_ready, item + 1)
                    nc.scalar.activation(tails[:, g, :], upre[:, g % 2, T + 1:T + KC], ACT.Copy)\
                        .then_inc(tails_saved, 1)
                elif p[0] == "xp":
                    ps, free = read(at, p)
                    wait(act, b_stored, c * 16)
                    nc.scalar.activation(dbc[:, :], ps[0:R + 2 * NS, :], ACT.Copy).then_inc(free, 1)
                yield

            def inv_sqrt(step0, dst, var):
                nc.scalar.activation(dst, var, ACT.Ln, bias=eps[:, :]).then_inc(rstd_step, 1)
                act.wait_ge(rstd_step, step0 + 1)
                nc.scalar.activation(dst, dst, ACT.Exp, scale=-0.5).then_inc(rstd_step, 1)

            def row_rstd(c, i):
                step0 = (c * NB + i) * 2
                act.wait_ge(ln_step, step0 + 2)
                inv_sqrt(step0 + 2, rstd[:, i % 2:i % 2 + 1], mv[:, i % 2, 1:2])

            def slot(k, s, mid, steps):
                dA_make(k, s, 0)
                dA_make(k, s, 1)
                for _ in mid:
                    pass
                dA_make(k, s, 2)
                dA_make(k, s, 3)
                for _ in steps:
                    pass

            def mid_of(c, at, s):
                for p in PLAN[s - 1]:
                    if p[0] == "z" or p[0] == "u" and p[1] % 2 and c is not None:
                        yield from evac(c, at, p)

            def steps_of(k, c, at, s):
                for p in PLAN[s]:
                    if p[0] in ("T", "xn") and c is not None:
                        yield from evac(c, at, p)
                for p in PLAN[s - 1]:
                    if p[0] == "M" and p[2] == 3 and c is not None:
                        row_rstd(c, p[1])
                        yield
                for p in PLAN[s - 2]:
                    if p[0] == "z" and k is not None:
                        yield from sigmoid(z_item(k, p[1]), gate, p[1])
                    if p[0] == "u" and c is not None:
                        yield from sigmoid(u_item(c, p[1]), u, p[1])
                for p in PLAN[s]:
                    if (p[0] == "u" and p[1] % 2 == 0 or p[0] == "xp") and c is not None:
                        yield from evac(c, at, p)
                    if p[0] == "dt" and p[1] < HG and c is not None:
                        dt_in(at, p[1])
                        yield
                if s == SLOTS - 1 and c is not None:
                    for g in range(HG):
                        softplus(c, g)

            def softplus(c, g):
                act.wait_ge(sp_clamped, c * G + g + 1)
                t = tmp[:, g % 4, :]
                nc.scalar.activation(t, t, ACT.Exp).then_inc(sp_step, 1)
                act.wait_ge(sp_step, (c * G + g) * 2 + 1)
                nc.scalar.activation(t, t, ACT.Ln, bias=1.0).then_inc(sp_step, 1)

            def dt_in(at, g):
                ps, free = read(at, ("dt", g))
                dst = vdt[:, g, :] if g < HG else delta[:, g, :]
                nc.scalar.activation(dst, ps[:, :], ACT.Identity, bias=bdt[:, g:g + 1]).then_inc(free, 1)

            def y_init(at, j):
                ps, free = read(at, ("uD", j))
                nc.scalar.activation(yT[:, j % NB, (j // NB) * T:(j // NB + 1) * T], ps[:, :], ACT.Copy)\
                    .then_inc(free, 1)

            def opening(c, at, first=False):
                dA_make(c, 0, 0)
                dA_make(c, 0, 1)
                wait(act, dA_ready, c * 128)
                for g in range(HG, G):
                    dt_in(at, g)
                dA_make(c, 0, 2)
                dA_make(c, 0, 3)
                for g in range(HG, G):
                    softplus(c, g)
                dA_make(c, 1, 0)
                dA_make(c, 1, 1)
                for j in range(NB):
                    y_init(at, j)
                dA_make(c, 1, 2)
                dA_make(c, 1, 3)
                for j in range(NB, 2 * NB):
                    y_init(at, j)
                for s in range(2, CUT):
                    slot(c, s, (), ())
                    if first and s - 2 < 4:
                        a = s - 2
                        w_evac(at, ("wo", a), WocT[:, 2 * a:2 * a + 2, :].rearrange("p a b -> p (a b)"))

            act.wait_ge(c_in, 8 * 16)
            act.wait_ge(eps_made, 1)
            nc.scalar.activation(Aneg[:, :, :], Aneg[:, :, :], ACT.Exp).then_inc(aneg_made, 1)
            act.wait_ge(aneg_made, 1)
            nc.scalar.activation(Aneg[:, :, :], Aneg[:, :, :], ACT.Copy, scale=-1.0).then_inc(aneg_made, 1)
            pro = part(None)
            for a in range(16):
                eb, mb = a // 4, a % 4
                w_evac(pro, ("wi", a), winT[mb // 2][:, mb % 2, eb * T:(eb + 1) * T])
            for a in range(2):
                w_evac(pro, ("wf", a), wfc2T[:, 2 * a:2 * a + 2, :].rearrange("p a b -> p (a b)"))
            w_evac(pro, ("wx", 0), WxT[:, :, :].rearrange("p a b -> p (a b)"))
            for a in range(2):
                w_evac(pro, ("wd", a), WdtT[:, a * T:(a + 1) * T], rows=R)
            for a in range(8):
                w_evac(pro, ("wc", a), WcT[:, a // 4, (a % 4) * T:(a % 4 + 1) * T])
            w_evac(pro, ("bc", 0), bc[:, :], cols=2 * G)
            act.wait_ge(hid_chain, 2 * JB)
            act.wait_ge(stt_done, STC)
            inv_sqrt(0, rstd[:, :], mv[:, :, 1])
            for p in FRONT0:
                if p[0] == "xp":
                    for g in range(G - 2, G):
                        for _ in sigmoid(u_item(0, g), u, g):
                            pass
                if p[0] == "M" and p[2] == 3:
                    row_rstd(0, p[1])
                for _ in evac(0, pro, p):
                    pass
                if p[0] == "dt" and p[1] < HG:
                    dt_in(pro, p[1])
                if p[0] == "u" and p[1] >= 2:
                    for _ in sigmoid(u_item(0, p[1] - 2), u, p[1] - 2):
                        pass
            for g in range(HG):
                softplus(0, g)
            act.wait_ge(aneg_made, 2)
            opening(0, pro, True)
            with act.Fori(0, NCH - 1) as k:
                at = part(k)
                for s in range(CUT, SLOTS):
                    slot(k, s, mid_of(k + 1, at, s), steps_of(k, k + 1, at, s))
                opening(k + 1, at)
            k = NCH - 1
            at = part(k)
            for s in range(CUT, SLOTS):
                slot(k, s, mid_of(None, at, s), steps_of(k, None, at, s))

        @block.vector
        def _(dve):
            def read(at, job):
                b, n = at(job)
                dve.wait_ge(misc_ready[b], n + 1)
                return misc[b], misc_free[b], n + 1

            nc.vector.memset(state[:, :, :], 0.0).then_inc(state_saved, SLOTS)
            nc.vector.memset(tails[:, :, :], 0.0).then_inc(tails_saved, G)
            nc.vector.memset(mv[:, :, :], 0.0).then_inc(scan_done, SC)
            nc.vector.memset(rstd[:, :], 0.0).then_inc(stt_done, STC)
            dve.wait_ge(x_in, 16)
            dve.wait_ge(c_in, 8 * 16)
            dve.wait_ge(scan_done, SC)
            for b in range(JB):
                if b >= 2:
                    dve.wait_ge(hid_chain, 2 * (b - 1))
                nc.vector.bn_stats(stats[:, b % 2, :], hid[:, b, :]).then_inc(hid_chain, 1)
                dve.wait_ge(hid_chain, 2 * b + 1)
                nc.vector.bn_aggr(mv[:, b, :], stats[:, b % 2, :]).then_inc(hid_chain, 1)
            dve.wait_ge(rstd_step, 2)
            for b in range(JB):
                nc.vector.tensor_scalar(hid[:, b, :], hid[:, b, :], mv[:, b, 0:1], rstd[:, b:b + 1],
                                        ALU.subtract, ALU.mult).then_inc(hid_made, 1)
            for b in range(JB):
                dve.wait_ge(hid_made, b + 1)
                nc.vector.tensor_tensor(hid[:, b, :], hid[:, b, :], Wbc, ALU.mult).then_inc(hid_made, 1)
            dve.wait_ge(hid_made, 2 * JB)
            dve.wait_ge(ident_made, 2)
            for g in range(G):
                nc.vector.tensor_scalar(diagD[:, g, :], ident[:, :], Dcol[:, g:g + 1], None, ALU.mult)\
                    .then_inc(diag_made, 1)

            def row_stats(c, at, i):
                ps, free, n = read(at, ("x1", i))
                r = i % 2
                base = (c * NB + i) * 2
                xr = x1new[:, i, :]
                dve.wait_ge(x_loaded, (c + 1) * 16)
                nc.vector.tensor_tensor(xr, ps[:, 0:D], xr, ALU.add).then_inc(free, 1)
                dve.wait_ge(free, n)
                wait(dve, ln_step, base - 2)
                nc.vector.bn_stats(stats[:, r, :], xr).then_inc(ln_step, 1)
                wait(dve, xn_made, c * NB + (i - 1))
                wait(dve, pad_set, c * NB + i)
                dve.wait_ge(ln_step, base + 1)
                nc.vector.memset(pad[:, :], 0.0).then_inc(pad_set, 1)
                nc.vector.bn_aggr(mv[:, r, :], stats[:, r, :]).then_inc(ln_step, 1)

            def normalize(c, at, i):
                r = i % 2
                xr = x1new[:, i, :]
                dve.wait_ge(rstd_step, (c * NB + i) * 2 + 4)
                if i < 2:
                    wait(dve, conv_step, c * G * 4)
                    dve.wait_ge(tails_saved, c * G + G)
                nc.vector.tensor_scalar(xn[i], xr, mv[:, r, 0:1], rstd[:, r:r + 1],
                                        ALU.subtract, ALU.mult).then_inc(xn_made, 1)
                dve.wait_ge(xn_made, c * NB + (i + 1))
                nc.vector.tensor_tensor(xr, xr, b2[:, :], ALU.add).then_inc(x1_made, 1)

            def clamp(item, tensor, g):
                nc.vector.tensor_scalar(tensor[:, g, :], tensor[:, g, :], SCLAMP, None, ALU.max)\
                    .then_inc(clamped, 1)

            def conv(c, at, g):
                base = (c * G + g) * 4
                b, n = at(("u", g))
                dve.wait_ge(misc_free[b], n + 1)
                dve.wait_ge(upre_ready, c * G + g + 1)
                src = upre[:, g % 2, :]
                nc.vector.tensor_scalar(u[:, g, :], src[:, KC:KC + T], cw[:, g, KC - 1:KC], cb[:, g:g + 1],
                                        ALU.mult, ALU.add).then_inc(conv_step, 1)
                for t in range(KC - 1):
                    dve.wait_ge(conv_step, base + t + 1)
                    nc.vector.scalar_tensor_tensor(u[:, g, :], src[:, 1 + t:1 + t + T], cw[:, g, t:t + 1],
                                                   u[:, g, :], ALU.mult, ALU.add).then_inc(conv_step, 1)
                dve.wait_ge(conv_step, base + 4)
                clamp(u_item(c, g), u, g)

            def scan(k, s, j):
                n, g = s // 2, (s % 2) * HG + j
                q = k * 128 + (s * 4 + j)
                dve.wait_ge(dA_ready, q + 1)
                dve.wait_ge(dBu_ready, q + 1)
                if j == 0:
                    wait(dve, hT_ready, k * 128 + (s * 4 - 4))
                    dve.wait_ge(state_saved, k * SLOTS + (s + SLOTS - 1))
                nc.vector.tensor_tensor_scan(h[:, s % 2, j, :], dA[j % 2][:, :], dBu[:, j, :],
                                             state[:, n, g:g + 1], ALU.mult, ALU.add).then_inc(scan_done, 1)

            def save_state(k, s):
                dve.wait_ge(scan_done, k * 128 + (s * 4 + 4 + SC))
                half = s % 2
                nc.vector.tensor_copy(state[:, s // 2, half * HG:(half + 1) * HG], h[:, half, :, T - 1])\
                    .then_inc(state_saved, 1)

            def weigh(k, s, b, at):
                n, half = s // 2, s % 2
                dve.wait_ge(hT_ready, k * 128 + (s * 4 + b + 1))
                if s < 2:
                    bk, m = at(("uD", half * NB + b))
                    dve.wait_ge(misc_free[bk], m + 1)
                else:
                    dve.wait_ge(stt_done, k * 128 + ((s - 2) * 4 + b + 1 + STC))
                y = yT[:, b, half * T:(half + 1) * T]
                nc.vector.scalar_tensor_tensor(y, hT[b][:, :], Ct[:, b, n:n + 1], y, ALU.mult, ALU.add)\
                    .then_inc(stt_done, 1)

            def slot(k, s, at, items, early=()):
                items = list(items)
                for f in early:
                    f()
                for j in range(HG):
                    scan(k, s, j)
                    if j == 1 and items:
                        items.pop(0)()
                if s:
                    save_state(k, s - 1)
                    for b in range(NB):
                        weigh(k, s - 1, b, at)
                        if b == 1 and items:
                            items.pop(0)()
                for f in items:
                    f()

            def front_items(k, c, at, s):
                if s == CUT + 1:
                    yield lambda: move_x1(k)
                for p in PLAN[s - 1]:
                    if p[0] == "z":
                        def z(g=p[1]):
                            b, n = at(("z", g))
                            dve.wait_ge(misc_free[b], n + 1)
                            clamp(z_item(k, g), gate, g)
                        if s != CUT + 1:
                            yield lambda: None
                        yield z
                    elif p[0] == "u" and c is not None:
                        yield lambda g=p[1]: conv(c, at, g)
                for p in PLAN[s - 1]:
                    if p[0] == "M" and p[2] == 3 and c is not None:
                        yield lambda i=p[1]: normalize(c, at, i)
                if s == SLOTS - 1 and c is not None:
                    yield lambda: None
                    yield lambda: None
                    for g in range(HG):
                        yield lambda g=g: top(c, g)

            def front_early(c, at, s):
                for p in PLAN[s - 1]:
                    if p[0] == "M" and p[2] == 3:
                        yield lambda i=p[1]: row_stats(c, at, i)
                    if p[0] == "dt":
                        yield lambda g=p[1]: cut(c, at, g)

            def close_scan(k, at_k):
                save_state(k, SLOTS - 1)
                for b in range(NB):
                    weigh(k, SLOTS - 1, b, at_k)

            def gate_y(k, at, g):
                ps, free, _ = read(at, ("y", g))
                dve.wait_ge(sig_used, z_item(k, g) + 1)
                nc.vector.tensor_tensor(gate[:, g, :], ps[:, :], gate[:, g, :], ALU.mult).then_inc(free, 1)

            def cut(c, at, g):
                b, n = at(("dt", g))
                dve.wait_ge(misc_free[b], n + 1)
                if g < HG:
                    dve.wait_ge(sig_used, u_item(c, G))
                else:
                    dve.wait_ge(delta_ready, c * G + (g - HG + 1))
                src = vdt if g < HG else delta
                nc.vector.tensor_scalar(tmp[:, g % 4, :], src[:, g, :], CLAMP, None, ALU.min)\
                    .then_inc(sp_clamped, 1)

            def top(c, g):
                dve.wait_ge(sp_step, (c * G + g) * 2 + 2)
                src = vdt if g < HG else delta
                if g < HG:
                    wait(dve, dBu_ready, c * 128 - HG)
                    wait(dve, dA_ready, c * 128 - HG)
                nc.vector.tensor_tensor(delta[:, g, :], src[:, g, :], tmp[:, g % 4, :], ALU.max)\
                    .then_inc(delta_ready, 1)

            def take_C(c, at):
                ps, free, n = read(at, ("ct", 0))
                dve.wait_ge(stt_done, c * 128 + STC)
                nc.vector.tensor_copy(Ct[:, :, :], ps[:, 0:NB * (R + 2 * NS)]
                                      .rearrange("p (b r) -> p b r", b=NB)[:, :, R + NS:]).then_inc(free, 1)
                dve.wait_ge(free, n)

            def opening(k, c, at):
                for j in range(2):
                    scan(c, 0, j)
                for g in range(HG, G):
                    cut(c, at, g)
                take_C(c, at)
                for j in range(2, HG):
                    scan(c, 0, j)
                for g in range(G):
                    if k is not None:
                        gate_y(k, at, g)
                    if g >= HG:
                        top(c, g)
                for s in range(1, CUT):
                    late = s >= 2 and s % 2 == 0 and k is not None
                    slot(c, s, at, [lambda b=s // 2 - 1: finish(k, at, b)] if late else ())
                if k is not None:
                    finish(k, at, NB - 1)

            def finish(k, at, b):
                if b == 0:
                    dve.wait_ge(x1_moved, k + 1)
                ps, free, _ = read(at, ("o", b))
                nc.vector.tensor_tensor(x1cur[:, b, :], ps[:, 0:D], x1cur[:, b, :], ALU.add).then_inc(free, 1)

            def move_x1(k):
                dve.wait_ge(x1_made, (k + 1) * NB)
                wait(dve, out_stored, k * 16)
                nc.vector.tensor_copy(x1cur[:, :, :], x1new[:, :, :]).then_inc(x1_moved, 1)

            pro = part(None)
            for p in FRONT0:
                if p[0] == "u":
                    conv(0, pro, p[1])
                elif p[0] == "M" and p[2] == 3:
                    row_stats(0, pro, p[1])
                    normalize(0, pro, p[1])
            for g in range(HG):
                cut(0, pro, g)
            for g in range(HG):
                top(0, g)
            opening(None, 0, pro)
            with dve.Fori(0, NCH - 1) as k:
                at = part(k)
                for s in range(CUT, SLOTS):
                    slot(k, s, at, front_items(k, k + 1, at, s), front_early(k + 1, at, s))
                close_scan(k, at)
                opening(k, k + 1, at)
            k = NCH - 1
            at = part(k)
            for s in range(CUT, SLOTS):
                slot(k, s, at, front_items(k, None, at, s))
            close_scan(k, at)
            for g in range(G):
                gate_y(k, at, g)
            for b in range(NB):
                finish(k, at, b)

        @block.tensor
        def _(pe):
            def bank(at, job):
                b, n = at(job)
                wait(pe, misc_free[b], n)
                return misc[b], misc_ready[b]

            def turn(dst, src):
                k_, m_ = src.shape[0], src.shape[1]
                return nc.tensor.transpose(dst, src, ident[0:k_, 0:k_])

            def piece(c, at, p):
                if p[0] == "T":
                    ps, ready = bank(at, p)
                    _, i, q = p
                    pe.wait_ge(adj_loaded[q // 2], (c * NB + i + 1) * 16)
                    for a in range(4):
                        col = (q % 2) * T + a * P
                        last = turn(ps[:, a * P:(a + 1) * P], adj_in[:, q // 2, col:col + P])
                    last.then_inc(ready, 1)
                elif p[0] == "M":
                    _, i, q = p
                    b, n = at(("x1", i))
                    if q == 0:
                        wait(pe, misc_free[b], n)
                    bt, nt = at(("T", i, q))
                    pe.wait_ge(misc_free[bt], nt + 1)
                    for a in range(4):
                        last = nc.tensor.matmul(misc[b][:, 0:D], adjT[:, q % 2, a, :], hid[:, q * 4 + a, :],
                                                start=(q == 0 and a == 0), stop=(q == 3 and a == 3))
                    if q == 3:
                        last.then_inc(misc_ready[b], 1)
                elif p[0] == "xn":
                    i = p[1]
                    ps, ready = bank(at, p)
                    pe.wait_ge(xn_made, c * NB + i + 1)
                    for a in range(2):
                        last = turn(ps[:, a * P:(a + 1) * P], xn[i][:, a * P:(a + 1) * P])
                    last.then_inc(ready, 1)
                elif p[0] in ("z", "u"):
                    g = p[1]
                    ps, ready = bank(at, p)
                    if p[0] == "u" and g == 0:
                        b, n = at(("xn", NB - 1))
                        pe.wait_ge(misc_free[b], n + 1)
                    col = (DI if p[0] == "z" else 0) + g * P
                    for a in range(2):
                        last = nc.tensor.matmul(ps[:, :], WcT[:, a, col:col + P], xnT[:, a, :],
                                                start=(a == 0), stop=(a == 1))
                    last.then_inc(ready, 1)
                elif p[0] == "xp":
                    ps, ready = bank(at, p)
                    for g in range(G):
                        pe.wait_ge(sig_used, u_item(c, g) + 1)
                        last = nc.tensor.matmul(ps[0:R + 2 * NS, :], WxT[:, g, :], u[:, g, :],
                                                start=(g == 0), stop=(g == G - 1))
                    last.then_inc(ready, 1)
                elif p[0] == "dt":
                    if p[1] == 0:
                        b, n = at(("xp",))
                        pe.wait_ge(misc_free[b], n + 1)
                    dt_job(at, p[1])

            def turn_h(k, s):
                half = s % 2
                pe.wait_ge(scan_done, k * 128 + (s * 4 + 4 + SC))
                for b in range(NB):
                    pe.wait_ge(stt_done, k * 128 + (s * 4 + b - 3 + STC))
                    for j in range(HG):
                        last = turn(hT[b][:, j * P:(j + 1) * P], h[:, half, j, b * P:(b + 1) * P])
                    last.then_inc(hT_ready, 1)

            def dt_job(at, g):
                ps, ready = bank(at, ("dt", g))
                nc.tensor.matmul(ps[:, :], WdtT[:, g * P:(g + 1) * P], dbc[0:R, :], start=True, stop=True)\
                    .then_inc(ready, 1)

            def y_job(at, g):
                ps, ready = bank(at, ("y", g))
                for b in range(NB):
                    last = turn(ps[:, b * P:(b + 1) * P], yT[:, b, g * P:(g + 1) * P])
                last.then_inc(ready, 1)

            def out_job(at, b):
                ps, ready = bank(at, ("o", b))
                for g in range(G):
                    last = nc.tensor.matmul(ps[:, 0:D], gate[:, g, b * P:(b + 1) * P], WocT[:, g, :],
                                            start=(g == 0), stop=(g == G - 1))
                last.then_inc(ready, 1)

            def boundary(k, c, at):
                for g in range(HG + 2, G):
                    dt_job(at, g)
                ps, ready = bank(at, ("ct", 0))
                w = R + 2 * NS
                for b in range(NB):
                    last = nc.tensor.matmul(ps[:, b * w:(b + 1) * w], dbc[:, b * P:(b + 1) * P],
                                            ident[0:w, 0:w], start=True, stop=True)
                last.then_inc(ready, 1)
                if k is not None:
                    turn_h(k, SLOTS - 1)
                    pe.wait_ge(stt_done, k * 128 + (128 + STC))
                    for g in range(G):
                        y_job(at, g)
                for j in range(2 * NB):
                    if j == NB:
                        turn_h(c, 0)
                    ps, ready = bank(at, ("uD", j))
                    b = j % NB
                    for a in range(HG):
                        g = (j // NB) * HG + a
                        last = nc.tensor.matmul(ps[:, a * P:(a + 1) * P], u[:, g, b * P:(b + 1) * P],
                                                diagD[:, g, :], start=True, stop=True)
                    last.then_inc(ready, 1)

            pro = part(None)
            pe.wait_ge(ident_made, 2)
            pe.wait_ge(w_first, 16)
            for a in range(16):
                ps, ready = bank(pro, ("wi", a))
                eb, mb = a // 4, a % 4
                if a == 8:
                    pe.wait_ge(w_in, 16 * 5)
                for e in range(4):
                    row = eb * 4 + e
                    last = turn(ps[:, e * P:(e + 1) * P], win[row // 8][:, row % 8, mb * P:(mb + 1) * P])
                last.then_inc(ready, 1)
            for a in range(2):
                ps, ready = bank(pro, ("wf", a))
                for e in range(4):
                    mb, ob = 2 * a + e // 2, e % 2
                    last = turn(ps[:, e * P:(e + 1) * P], wfc2[:, ob, mb * P:(mb + 1) * P])
                last.then_inc(ready, 1)
            ps, ready = bank(pro, ("wx", 0))
            w = R + 2 * NS
            for g in range(G):
                last = turn(ps[:, g * w:(g + 1) * w], wxp[:, g * P:(g + 1) * P])
            last.then_inc(ready, 1)
            for a in range(2):
                ps, ready = bank(pro, ("wd", a))
                for e in range(4):
                    last = nc.tensor.matmul(ps[0:R, e * P:(e + 1) * P], wdt[:, a * 4 + e, :], ident[:, :],
                                            start=True, stop=True)
                last.then_inc(ready, 1)
            b, n = pro(("wi", 15))
            pe.wait_ge(misc_free[b], n + 1)
            b, n = pro(("wi", 14))
            pe.wait_ge(misc_free[b], n + 1)
            for a in range(8):
                ps, ready = bank(pro, ("wc", a))
                ib, eb = a // 4, a % 4
                for mb in range(4):
                    last = nc.tensor.matmul(ps[:, :], wfc1[:, mb, ib * P:(ib + 1) * P],
                                            winT[mb // 2][:, mb % 2, eb * T:(eb + 1) * T],
                                            start=(mb == 0), stop=(mb == 3))
                last.then_inc(ready, 1)
            ps, ready = bank(pro, ("bc", 0))
            pe.wait_ge(c_in, 8 * 16)
            for e in range(2 * G):
                for mb in range(4):
                    last = nc.tensor.matmul(ps[:, e:e + 1], winT[mb // 2][:, mb % 2, e * P:(e + 1) * P],
                                            bf1[:, mb:mb + 1], start=(mb == 0), stop=(mb == 3))
            last.then_inc(ready, 1)
            pe.wait_ge(hid_made, 2 * JB)
            for p in FRONT0:
                if p[0] == "u" and p[1] == 0:
                    for name in (("bc", 0), ("wc", 7), ("wc", 6)):
                        b, n = pro(name)
                        pe.wait_ge(misc_free[b], n + 1)
                piece(0, pro, p)
            pe.wait_ge(diag_made, G)
            boundary(None, 0, pro)
            for s in range(2, CUT):
                turn_h(0, s - 1)
                if s == 2:
                    pe.wait_ge(w_out, 16)
                if s - 2 < 4:
                    a = s - 2
                    ps, ready = bank(pro, ("wo", a))
                    for e in range(2):
                        g = 2 * a + e
                        for mb in range(4):
                            last = nc.tensor.matmul(ps[:, e * D:(e + 1) * D], wout[:, mb, g * P:(g + 1) * P],
                                                    wfc2T[:, mb, :], start=(mb == 0), stop=(mb == 3))
                    last.then_inc(ready, 1)
            with pe.Fori(0, NCH - 1) as k:
                at = part(k)
                for s in range(CUT, SLOTS):
                    turn_h(k, s - 1)
                    for p in PLAN[s]:
                        piece(k + 1, at, p)
                boundary(k, k + 1, at)
                for s in range(1, CUT):
                    if s > 1:
                        turn_h(k + 1, s - 1)
                    if s % 2:
                        out_job(at, s // 2)
            k = NCH - 1
            at = part(k)
            for s in range(CUT, SLOTS):
                turn_h(k, s - 1)
                for p in PLAN[s]:
                    if p[0] == "z":
                        piece(None, at, p)
            turn_h(k, SLOTS - 1)
            pe.wait_ge(stt_done, k * 128 + 128 + STC)
            for g in range(G):
                y_job(at, g)
            b, n = at(("y", G - 1))
            pe.wait_ge(misc_free[b], n + 1)
            for b in range(NB):
                out_job(at, b)


_INS = ['x', 'adj', 'L0_gnn_W', 'L0_ffn_W_fc1', 'L0_ffn_b_fc1', 'L0_ffn_W_in', 'L0_ffn_conv_w', 'L0_ffn_conv_b',
        'L0_ffn_W_xproj', 'L0_ffn_W_dt', 'L0_ffn_b_dt', 'L0_ffn_A_log', 'L0_ffn_D', 'L0_ffn_W_out',
        'L0_ffn_W_fc2', 'L0_ffn_b_fc2']


def kernel(**inputs):
    import numpy as _np
    import concourse.bacc as _bacc
    from concourse import mybir as _mybir
    from concourse.bass_utils import run_bass_kernel_spmd as _run

    nc = _bacc.Bacc("TRN2", target_bir_lowering=False, num_devices=1)
    arrays, args = {}, []
    for name in _INS:
        a = _np.ascontiguousarray(inputs[name])
        arrays[f"in_{name}"] = a
        args.append(nc.dram_tensor(f"in_{name}", a.shape, _mybir.dt.from_np(a.dtype), kind="ExternalInput").ap())
    args.append(nc.dram_tensor("out_0", (N, D), _mybir.dt.float32, kind="ExternalOutput").ap())
    build(nc, *args)
    r = _run(nc, [arrays], core_ids=[0])
    return r.results[0]["out_0"]
```

```python
import concourse.bass as bass
from concourse import mybir
from contextlib import ExitStack

P = 128
N = 2048
D = 256
DM = 512
DI = 1024
NS = 16
R = 32
KC = 4
T = 512
NCH = N // T
NB = T // P
JB = N // P
G = DI // P
HG = G // 2
SLOTS = 2 * NS
CUT = 8
CLAMP = 30.0
SCLAMP = 40.0
EPS = 1e-5


def front_plan():
    quarters = [(i, q) for i in range(NB) for q in range(4)]
    plan = {s: [] for s in range(SLOTS)}
    slot_of = [CUT + 3 * (a // 4) + min(a % 4, 2) for a in range(4 * NB)]
    for a, (i, q) in enumerate(quarters):
        s = slot_of[a]
        plan[s].append(("T", i, q))
        if a:
            plan[s].append(("M",) + quarters[a - 1])
        if a % 4 < 2:
            plan[s].append(("z", a // 4 * 2 + a % 4))
    plan[20].append(("M",) + quarters[-1])
    where = {p: s for s in plan for p in plan[s]}
    assert all(where[("M", i, 3)] < where[("M", i + 1, 0)] for i in range(NB - 1))
    for i in range(NB):
        plan[max(where[("M", i, 3)] + 2, where[("z", G - 1)] + 1 + i)].insert(0, ("xn", i))
    first = where[("M", NB - 1, 3)] + 2
    for g in range(G):
        plan[first + g // 2].append(("u", g))
    last = first + (G - 1) // 2
    for g in range(G):
        plan[last + 1 + max(g // 2, 1)].append(("xp", g))
    for g in range(HG + 2):
        plan[last + 4 + g // 2].append(("dt", g))
    assert last + 6 == SLOTS - 1
    return plan


def bank_of(job):
    kind = job[0]
    if kind in ("x1", "xp", "ct"):
        return 0
    if kind in ("T", "z", "xn"):
        return 1
    return job[-1] % 2


def jobs_of(pieces):
    for p in pieces:
        if p[0] == "M":
            if p[2] == 0:
                yield ("x1", p[1])
        elif p[0] == "xp":
            if p[1] == 0:
                yield ("xp",)
        else:
            yield p


def numbered(jobs):
    count, out = [0, 0], {}
    for j in jobs:
        b = bank_of(j)
        assert j not in out
        out[j] = (b, count[b])
        count[b] += 1
    return out, count


def build(nc, x, adj, gnnW, W_fc1, b_fc1, W_in, conv_w, conv_b, W_xp, W_dt, b_dt, A_log, Dp, W_out, W_fc2,
          b_fc2, out):
    f32 = mybir.dt.float32
    ALU = mybir.AluOpType
    ACT = mybir.ActivationFunctionType

    PLAN = front_plan()
    FRONT = [p for s in range(SLOTS) for p in PLAN[s]]
    FRONT0 = [p for p in FRONT if p[0] != "z"]
    Z_LAST = [p for p in FRONT if p[0] == "z"]
    WEIGHTS = ([("wi", a) for a in range(8)] + [("wc", a) for a in range(4)]
               + [("wi", a) for a in range(8, 16)] + [("wf", a) for a in range(2)] + [("wx", 0)]
               + [("wd", a) for a in range(2)] + [("wc", a) for a in range(4, 8)])
    DT = [("dt", g) for g in range(HG + 2, G)]
    Y = [("y", g) for g in range(G)]
    UD = [("uD", j) for j in range(2 * NB)]
    OUTJ = [("o", b) for b in range(NB)]
    PRO, PRO_N = numbered(WEIGHTS + list(jobs_of(FRONT0)) + DT + [("ct", 0)] + UD + [("wo", a) for a in range(4)])
    LOOP, LOOP_N = numbered(list(jobs_of(FRONT)) + DT + [("ct", 0)] + Y + UD + OUTJ)
    EPI, _ = numbered(Z_LAST + Y + OUTJ)

    def part(k):
        if k is None:
            return lambda job: (PRO[job][0], PRO[job][1])
        jobs = EPI if isinstance(k, int) and k == NCH - 1 else LOOP

        def at(job):
            b, n = jobs[job]
            return b, k * LOOP_N[b] + (PRO_N[b] + n)
        return at

    def wait(eng, sem, value):
        if isinstance(value, int) and value <= 0:
            return
        eng.wait_ge(sem, value)

    ctx = ExitStack()
    with ctx:
        def sb(name, shape):
            return ctx.enter_context(nc.sbuf_tensor(name, shape, f32))

        def pb(name, shape):
            return ctx.enter_context(nc.psum_tensor(name, shape, f32))

        def sem(name):
            return ctx.enter_context(nc.semaphore(name))

        Bscr = nc.dram_tensor("B_rows", [NCH, NS, T], f32, kind="Internal").ap()

        ident = sb("ident", [P, P])
        eps = sb("eps", [P, 1])
        sclamp = sb("sclamp", [P, 1])
        pad = sb("pad", [P, 1])
        hid = sb("hid", [P, JB, D])
        WcT = sb("WcT", [P, 2, 2 * DI])
        WocT = sb("WocT", [P, G, D])
        WxT = sb("WxT", [P, G, R + 2 * NS])
        WdtT = sb("WdtT", [R, DI])
        diagD = sb("diagD", [P, G, P])
        Aneg = sb("Aneg", [P, G, NS])
        cw = sb("cw", [P, G, KC])
        cb = sb("cb", [P, G])
        bdt = sb("bdt", [P, G])
        Dcol = sb("Dcol", [P, G])
        bias_share = sb("bias_share", [P, G])
        bc = sb("bc", [P, 2 * G])
        b2 = sb("b2", [P, D])
        adj_in = sb("adj_in", [P, 2, N // 2])
        adjT = sb("adjT", [P, 2, 4, P])
        x1new = sb("x1new", [P, NB, D])
        x1cur = sb("x1cur", [P, NB, D])
        stats = sb("stats", [P, 2, 6])
        mv = sb("mv", [P, JB, 2])
        rstd = sb("rstd", [P, JB])
        xnT = sb("xnT", [P, 2, T])
        upre = sb("upre", [P, 2, T + KC])
        tails = sb("tails", [P, G, KC - 1])
        tmp = sb("tmp", [P, 4, T])
        dbc = sb("dbc", [R + 2 * NS, T])
        Ct = sb("Ct", [P, NB, NS])
        state = sb("state", [P, NS, G])
        h = sb("h", [P, 2, HG, T])
        yT = sb("yT", [P, NB, DI])
        delta = sb("delta", [P, G, T])
        du = sb("du", [P, G, T])
        gate = sb("gate", [P, G, T])
        u = sb("u", [P, G, T])
        Bbc = sb("Bbc", [P, 4, T])
        dBu = sb("dBu", [P, 4, T])
        xn = [upre[:, i % 2, KC + i // 2 * D:KC + (i // 2 + 1) * D] for i in range(NB)]
        vdt = adj_in[:, :, :].rearrange("p a (b t) -> p (a b) t", t=T)
        win = [h[:, :, :, :].rearrange("p a b t -> p (a b) t"),
               yT[:, :, :].rearrange("p b (c t) -> p (b c) t", t=DM)]
        winT = [delta[:, :, :].rearrange("p (m c) t -> p m (c t)", m=2),
                du[:, :, :].rearrange("p (m c) t -> p m (c t)", m=2)]
        wout = gate[:, :, :].rearrange("p (m c) t -> p m (c t)", m=4)
        wfc1 = u[:, 0:2, :].rearrange("p a (b t) -> p (a b) t", b=2)
        wfc2 = u[:, 2:4, :]
        wfc2T = x1cur
        wdt = u[:, 6, 0:G * R].rearrange("p (g r) -> p g r", r=R)
        wxp = Bbc[0:R + 2 * NS, 0:2, :].rearrange("p a t -> p (a t)")
        Wbc = dBu[:, 0, 0:D]
        bf1 = dBu[:, 1, :]
        products = [dBu[:, 2 + i, :] for i in range(2)]

        dA = [pb(f"dA{i}", [P, T]) for i in range(2)]
        hT = [pb(f"hT{i}", [P, T]) for i in range(4)]
        misc = [pb(f"misc{i}", [P, T]) for i in range(2)]

        misc_ready = [sem(f"misc{i}_ready") for i in range(2)]
        misc_free = [sem(f"misc{i}_free") for i in range(2)]
        ident_made = sem("ident_made")
        pad_set = sem("pad_set")
        eps_made = sem("eps_made")
        x_in = sem("x_in")
        w_quarter = sem("w_quarter")
        w_first = sem("w_first")
        w_in = sem("w_in")
        w_out = sem("w_out")
        bc_made = sem("bc_made")
        rows_in = sem("rows_in")
        c_in = sem("c_in")
        hid_chain = sem("hid_chain")
        hid_made = sem("hid_made")
        aneg_made = sem("aneg_made")
        diag_made = sem("diag_made")
        adj_loaded = [sem(f"adj_loaded{i}") for i in range(2)]
        x_loaded = sem("x_loaded")
        ln_step = sem("ln_step")
        rstd_step = sem("rstd_step")
        xn_made = sem("xn_made")
        x1_made = sem("x1_made")
        x1_moved = sem("x1_moved")
        upre_ready = sem("upre_ready")
        tails_saved = sem("tails_saved")
        conv_step = sem("conv_step")
        relu_made = sem("relu_made")
        sig_step = sem("sig_step")
        sig_used = sem("sig_used")
        b_stored = sem("b_stored")
        b_loaded = [sem(f"b_loaded{i}") for i in range(4)]
        sp_clamped = sem("sp_clamped")
        sp_step = sem("sp_step")
        delta_ready = sem("delta_ready")
        du_ready = sem("du_ready")
        dA_ready = sem("dA_ready")
        dBu_ready = sem("dBu_ready")
        scan_done = sem("scan_done")
        state_saved = sem("state_saved")
        hT_ready = sem("hT_ready")
        stt_done = sem("stt_done")
        out_stored = sem("out_stored")

        SC = 4
        STC = 4

        block = ctx.enter_context(nc.Block())

        def z_item(k, g):
            return k * 16 + (8 + g)

        def u_item(c, g):
            return c * 16 + g

        def sig_steps(item):
            return item * 3 if isinstance(item, int) and item < G else item * 4 - G

        @block.sync
        def _(sp):
            def adj_load(c, i, hf, at):
                if i:
                    b, n = at(("T", i - 1, 2 * hf + 1))
                    sp.wait_ge(misc_ready[b], n + 1)
                else:
                    wait(sp, delta_ready, c * G - HG)
                rows = bass.ts(c * NB + i, P)
                sp.dma_start(adj_in[:, hf, :], adj[rows, hf * (N // 2):(hf + 1) * (N // 2)])\
                    .then_inc(adj_loaded[hf], 16)

            def b_load(c, n, k_before, n_before):
                if n_before is not None:
                    used = k_before * 128 + (n_before + 1) * G
                    if n == 0 and not isinstance(c, int):
                        used = sp.to_reg(used)
                if n == 0:
                    sp.wait_ge(b_stored, (c + 1) * 16)
                if n_before is not None:
                    sp.wait_ge(dBu_ready, used)
                sp.dma_start(Bbc[:, n % 4, :], Bscr[c, n, :].partition_broadcast(P) if isinstance(c, int)
                             else Bscr[bass.ds(c, 1), n, :].rearrange("a t -> (a t)").partition_broadcast(P))\
                    .then_inc(b_loaded[n % 4], 16)

            def x_load(c):
                wait(sp, x1_moved, c)
                sp.dma_start(x1new[:, :, :], x[bass.ts(c, T), :].rearrange("(b p) d -> p b d", p=P))\
                    .then_inc(x_loaded, 16)

            def b_store(c, at):
                b, n = at(("xp",))
                sp.wait_ge(misc_free[b], n + 1)
                dst = Bscr[c, :, :] if isinstance(c, int) else Bscr[bass.ds(c, 1), :, :].rearrange("a n t -> (a n) t")
                sp.dma_start(dst, dbc[R:R + NS, :]).then_inc(b_stored, 16)

            def slot_loads(k, s):
                if s % 2 == 0 and 0 < s and s // 2 + 3 < NS:
                    b_load(k, s // 2 + 3, k, s // 2 - 1)

            def front_loads(c, at, pieces):
                for p in pieces:
                    if p[0] == "T" and p[2] % 2 and p[1] + 1 < NB:
                        adj_load(c, p[1] + 1, p[2] // 2, at)

            def w_load(dst, src, done):
                sp.dma_start(dst, src).then_inc(done, 16)

            def blocks(w):
                return w.rearrange("(b p) m -> p b m", p=P)

            w_load(win[0][:, 0:4, :], blocks(W_in[0:DI // 2, :]), w_quarter)
            w_load(win[0][:, 4:8, :], blocks(W_in[DI // 2:DI, :]), w_first)
            w_load(wfc1, blocks(W_fc1), w_first)
            w_load(win[1], blocks(W_in[DI:2 * DI, :]), w_in)
            w_load(wxp, W_xp, w_in)
            w_load(wdt, blocks(W_dt), w_in)
            w_load(wfc2, blocks(W_fc2), w_in)
            w_load(hid[:, :, :], blocks(x), x_in)
            adj_load(0, 0, 0, None)
            adj_load(0, 0, 1, None)
            x_load(0)
            w_load(wout, blocks(W_out), w_out)
            pro = part(None)
            front_loads(0, pro, FRONT0)
            b_store(0, pro)
            for n in range(4):
                b_load(0, n, 0, None)

            def opening(c):
                for s in range(CUT):
                    slot_loads(c, s)

            opening(0)

            def store_out(k, at):
                bk, n = at(("o", NB - 1))
                sp.wait_ge(misc_free[bk], n + 1)
                sp.dma_start(out[bass.ts(k, T), :].rearrange("(b p) d -> p b d", p=P), x1cur[:, :, :])\
                    .then_inc(out_stored, 16)

            with sp.Fori(0, NCH - 1) as k:
                at = part(k)
                adj_load(k + 1, 0, 0, at)
                adj_load(k + 1, 0, 1, at)
                for s in range(CUT, SLOTS):
                    if s == CUT + 2:
                        x_load(k + 1)
                    slot_loads(k, s)
                    front_loads(k + 1, at, PLAN[s])
                b_store(k + 1, at)
                for n in range(4):
                    b_load(k + 1, n, k, NS - 4 + n)
                opening(k + 1)
                store_out(k, at)
            k = NCH - 1
            for s in range(CUT, SLOTS):
                slot_loads(k, s)
            store_out(k, part(k))
            sp.wait_ge(out_stored, NCH * 16)

        @block.gpsimd
        def _(pool):
            slow = nc.allow_non_contiguous_dma(reason="one value per channel, once")
            ctx.enter_context(slow)
            pool.dma_start(bf1, b_fc1.partition_broadcast(P)).then_inc(rows_in, 16)
            pool.dma_start(Wbc, gnnW.partition_broadcast(P)).then_inc(rows_in, 16)
            pool.dma_start(b2[:, :], b_fc2.partition_broadcast(P)).then_inc(c_in, 16)
            pool.dma_start(cb[:, :], conv_b.rearrange("(b p) -> p b", p=P)).then_inc(c_in, 16)
            pool.dma_start(bdt[:, :], b_dt.rearrange("(b p) -> p b", p=P)).then_inc(c_in, 16)
            pool.dma_start(Dcol[:, :], Dp.rearrange("(b p) -> p b", p=P)).then_inc(c_in, 16)
            pool.dma_start(cw[:, :, :], conv_w.rearrange("(b p) m -> p b m", p=P)).then_inc(c_in, 16)
            pool.dma_start(Aneg[:, :, :], A_log.rearrange("(b p) m -> p b m", p=P)).then_inc(c_in, 16)
            nc.gpsimd.memset(eps[:, :], EPS).then_inc(eps_made, 1)
            nc.gpsimd.memset(sclamp[:, :], SCLAMP).then_inc(eps_made, 1)
            nc.gpsimd.memset(ident[:, :], 0.0).then_inc(ident_made, 1)
            pool.wait_ge(ident_made, 1)
            nc.gpsimd.affine_select(out=ident[:, :], in_=ident[:, :], compare_op=ALU.not_equal, fill=1.0,
                                    base=0, pattern=[[-1, P]], channel_multiplier=1).then_inc(ident_made, 1)

            def sig_use(item, tensor, g):
                pool.wait_ge(sig_step, sig_steps(item + 1))
                nc.gpsimd.tensor_tensor(tensor[:, g, :], tensor[:, g, :], tmp[:, g % 4, :], ALU.mult)\
                    .then_inc(sig_used, 1)

            def du_make(c, g):
                pool.wait_ge(delta_ready, c * G + g + 1)
                pool.wait_ge(sig_used, u_item(c, g) + 1)
                nc.gpsimd.tensor_tensor(du[:, g, :], delta[:, g, :], u[:, g, :], ALU.mult).then_inc(du_ready, 1)

            def dBu_make(k, s, j):
                n, g = s // 2, (s % 2) * HG + j
                q = k * 128 + (s * 4 + j)
                if j == 0:
                    pool.wait_ge(b_loaded[n % 4], k * 64 + (n // 4 + 1) * 16)
                if s < 2:
                    pool.wait_ge(du_ready, k * G + g + 1)
                pool.wait_ge(scan_done, q + (SC - 3))
                nc.gpsimd.tensor_tensor(dBu[:, j, :], du[:, g, :], Bbc[:, n % 4, :], ALU.mult)\
                    .then_inc(dBu_ready, 1)

            def slot(k, s, items):
                items = list(items)
                for j in range(HG):
                    dBu_make(k, s, j)
                    if j % 2 and items:
                        items.pop(0)()

            def front_items(k, c, s):
                for p in PLAN[s - 4]:
                    if p[0] == "z":
                        yield lambda g=p[1]: sig_use(z_item(k, g), gate, g)
                for p in PLAN[s - 3]:
                    if p[0] == "u" and c is not None:
                        yield lambda g=p[1]: sig_use(u_item(c, g), u, g)

            def opening(c):
                wait(pool, dBu_ready, c * 128)
                for g in range(G):
                    du_make(c, g)
                    dBu_make(c, g // HG, g % HG)
                for s in range(2, CUT):
                    slot(c, s, ())

            for g in range(G):
                sig_use(u_item(0, g), u, g)
            opening(0)
            with pool.Fori(0, NCH - 1) as k:
                for s in range(CUT, SLOTS):
                    slot(k, s, front_items(k, k + 1, s))
                opening(k + 1)
            for s in range(CUT, SLOTS):
                slot(NCH - 1, s, front_items(NCH - 1, None, s))

        @block.scalar
        def _(act):
            nc.scalar.preload_act_table_set("natural_log_exp_and_others")

            def read(at, job):
                b, n = at(job)
                act.wait_ge(misc_ready[b], n + 1)
                return misc[b], misc_free[b]

            def w_evac(at, job, dst, view=None, rows=P, cols=T):
                ps, free = read(at, job)
                src = ps[0:rows, 0:cols] if view is None else view(ps)
                nc.scalar.activation(dst, src, ACT.Copy).then_inc(free, 1)

            def dA_make(k, s, j):
                n, g = s // 2, (s % 2) * HG + j
                q = k * 128 + (s * 4 + j)
                if s < 2:
                    act.wait_ge(delta_ready, k * G + g + 1)
                act.wait_ge(scan_done, q + (SC - 1))
                nc.scalar.activation(dA[j % 2][:, :], delta[:, g, :], ACT.Exp, scale=Aneg[:, g, n:n + 1])\
                    .then_inc(dA_ready, 1)

            def sigmoid(c, g, at, kind, halves=(0, 1)):
                tensor, item = (gate, z_item(c, g)) if kind == "z" else (u, u_item(c, g))
                t = tmp[:, g % 4, :]
                count = sig_steps(item)
                if 0 not in halves:
                    count = count + 1
                elif kind == "u" and isinstance(c, int):
                    act.wait_ge(relu_made, g + 1)
                else:
                    if kind == "u":
                        act.wait_ge(conv_step, (c * G + g) * 3 + 3)
                    else:
                        b, n = at(("z", g))
                        act.wait_ge(misc_free[b], n + 1)
                    act.wait_ge(sig_used, item - 3)
                    nc.scalar.activation(t, tensor[:, g, :], ACT.Relu, bias=sclamp[:, :]).then_inc(sig_step, 1)
                    yield
                    count = count + 1
                    act.wait_ge(sig_step, count)
                if 0 in halves:
                    nc.scalar.activation(t, t, ACT.Exp, scale=-1.0, bias=sclamp[:, :]).then_inc(sig_step, 1)
                    yield
                if 1 not in halves:
                    return
                act.wait_ge(sig_step, count + 1)
                nc.scalar.activation(t, t, ACT.Ln, bias=1.0).then_inc(sig_step, 1)
                yield
                act.wait_ge(sig_step, count + 2)
                nc.scalar.activation(t, t, ACT.Exp, scale=-1.0).then_inc(sig_step, 1)
                yield

            def evac(c, at, p):
                if p[0] == "T":
                    ps, free = read(at, p)
                    nc.scalar.activation(adjT[:, p[2] % 2, :, :].rearrange("p a b -> p (a b)"), ps[:, :],
                                         ACT.Copy).then_inc(free, 1)
                elif p[0] == "xn":
                    ps, free = read(at, p)
                    nc.scalar.activation(xnT[:, :, p[1] * P:(p[1] + 1) * P],
                                         ps[:, 0:2 * P].rearrange("p (a b) -> p a b", a=2),
                                         ACT.Copy).then_inc(free, 1)
                elif p[0] == "z":
                    ps, free = read(at, p)
                    nc.scalar.activation(gate[:, p[1], :], ps[:, :], ACT.Identity,
                                         bias=bc[:, G + p[1]:G + p[1] + 1]).then_inc(free, 1)
                elif p[0] == "u":
                    g = p[1]
                    item = c * G + g
                    wait(act, conv_step, (item - 2) * 3 + 3)
                    act.wait_ge(tails_saved, item + (G - 1))
                    nc.scalar.activation(upre[:, g % 2, 1:KC], tails[:, g, :], ACT.Copy).then_inc(upre_ready, 1)
                    ps, free = read(at, p)
                    nc.scalar.activation(upre[:, g % 2, KC:KC + T], ps[:, :], ACT.Identity,
                                         bias=bc[:, g:g + 1]).then_inc(upre_ready, 1)
                    nc.scalar.activation(u[:, g, :], ps[:, :], ACT.Identity, scale=cw[:, g, KC - 1:KC],
                                         bias=cb[:, g:g + 1]).then_inc(free, 1)
                    act.wait_ge(upre_ready, 2 * item + 2)
                    nc.scalar.activation(tails[:, g, :], upre[:, g % 2, T + 1:T + KC], ACT.Copy)\
                        .then_inc(tails_saved, 1)
                elif p == ("xp", G - 1):
                    ps, free = read(at, ("xp",))
                    wait(act, b_stored, c * 16)
                    nc.scalar.activation(dbc[:, :], ps[0:R + 2 * NS, :], ACT.Copy).then_inc(free, 1)
                elif p[0] == "dt" and p[1] < HG:
                    dt_in(at, p[1])
                yield

            def inv_sqrt(step0, dst, var):
                nc.scalar.activation(dst, var, ACT.Ln, bias=eps[:, :]).then_inc(rstd_step, 1)
                act.wait_ge(rstd_step, step0 + 1)
                nc.scalar.activation(dst, dst, ACT.Exp, scale=-0.5).then_inc(rstd_step, 1)

            def row_rstd(c, i):
                step0 = (c * NB + i) * 2
                act.wait_ge(ln_step, step0 + 2)
                inv_sqrt(step0 + 2, rstd[:, i % 2:i % 2 + 1], mv[:, i % 2, 1:2])

            def slot(k, s, mid, steps):
                dA_make(k, s, 0)
                dA_make(k, s, 1)
                for _ in mid:
                    pass
                dA_make(k, s, 2)
                dA_make(k, s, 3)
                for _ in steps:
                    pass

            def ends_slot(p, s):
                if p[0] == "T":
                    return [q for q in PLAN[s] if q[0] == "T"].index(p) == 1
                return p[0] == "z" or p[0] == "u" and p[1] % 2 == 1 or p[0] == "dt" and p[1] < HG

            def mid_of(k, c, at, s):
                for p in PLAN[s - 3]:
                    if p[0] == "z":
                        yield from sigmoid(k, p[1], at, "z", (1,))
                for p in PLAN[s - 1]:
                    if ends_slot(p, s - 1) and (p[0] == "z" or c is not None):
                        yield from evac(c, at, p)

            def steps_of(k, c, at, s):
                for p in PLAN[s]:
                    if p[0] in ("T", "xn") and not ends_slot(p, s) and c is not None:
                        yield from evac(c, at, p)
                for p in PLAN[s - 1]:
                    if p[0] == "M" and p[2] == 3 and c is not None:
                        row_rstd(c, p[1])
                        yield
                for p in PLAN[s - 2]:
                    if p[0] == "z" and k is not None:
                        yield from sigmoid(k, p[1], at, "z", (0,))
                    if p[0] == "u" and c is not None:
                        yield from sigmoid(c, p[1], at, "u")
                for p in PLAN[s]:
                    if (p[0] == "u" and p[1] % 2 == 0 or p == ("xp", G - 1)) and c is not None:
                        yield from evac(c, at, p)
                    if p[0] == "dt" and p[1] < HG and not ends_slot(p, s) and c is not None:
                        yield from evac(c, at, p)
                if s >= SLOTS - 2 and c is not None:
                    for g in range(2):
                        softplus(c, (s - SLOTS + 2) * 2 + g)

            def softplus(c, g):
                act.wait_ge(sp_clamped, c * G + g + 1)
                t = tmp[:, g % 4, :]
                nc.scalar.activation(t, t, ACT.Exp).then_inc(sp_step, 1)
                act.wait_ge(sp_step, (c * G + g) * 2 + 1)
                nc.scalar.activation(t, t, ACT.Ln, bias=1.0).then_inc(sp_step, 1)

            def dt_in(at, g):
                ps, free = read(at, ("dt", g))
                dst = vdt[:, g, :] if g < HG else delta[:, g, :]
                nc.scalar.activation(dst, ps[:, :], ACT.Identity, bias=bdt[:, g:g + 1]).then_inc(free, 1)

            def y_init(at, j):
                ps, free = read(at, ("uD", j))
                nc.scalar.activation(yT[:, j % NB, (j // NB) * T:(j // NB + 1) * T], ps[:, :], ACT.Copy)\
                    .then_inc(free, 1)

            def opening(c, at, first=False):
                dA_make(c, 0, 0)
                dA_make(c, 0, 1)
                wait(act, dA_ready, c * 128)
                for g in range(HG, G):
                    dt_in(at, g)
                softplus(c, HG)
                dA_make(c, 0, 2)
                dA_make(c, 0, 3)
                for g in range(HG + 1, G):
                    softplus(c, g)
                dA_make(c, 1, 0)
                dA_make(c, 1, 1)
                for j in range(NB):
                    y_init(at, j)
                dA_make(c, 1, 2)
                dA_make(c, 1, 3)
                for j in range(NB, 2 * NB):
                    y_init(at, j)
                for s in range(2, CUT):
                    slot(c, s, (), ())
                    if first and s - 2 < 4:
                        a = s - 2
                        w_evac(at, ("wo", a), WocT[:, 2 * a:2 * a + 2, :].rearrange("p a b -> p (a b)"))

            pro = part(None)

            def half_of_W_in(half):
                for a in range(half * 8, half * 8 + 8):
                    eb, mb = a // 4, a % 4
                    w_evac(pro, ("wi", a), winT[mb // 2][:, mb % 2, eb * T:(eb + 1) * T])

            def half_of_product(half):
                for a in range(half * 4, half * 4 + 4):
                    w_evac(pro, ("wc", a), WcT[:, a % 2, (a // 2) * T:(a // 2 + 1) * T])

            half_of_W_in(0)
            half_of_product(0)
            half_of_W_in(1)
            for a in range(2):
                w_evac(pro, ("wf", a), wfc2T[:, 2 * a:2 * a + 2, :].rearrange("p a b -> p (a b)"))
            w_evac(pro, ("wx", 0), WxT[:, :, :].rearrange("p a b -> p (a b)"))
            for a in range(2):
                w_evac(pro, ("wd", a), WdtT[:, a * T:(a + 1) * T], rows=R)
            act.wait_ge(hid_chain, 2 * JB)
            act.wait_ge(stt_done, STC)
            act.wait_ge(eps_made, 2)
            inv_sqrt(0, rstd[:, :], mv[:, :, 1])
            half_of_product(1)
            act.wait_ge(bc_made, 4 * G)
            act.wait_ge(diag_made, 2)
            act.wait_ge(c_in, 6 * 16)
            nc.scalar.activation(Aneg[:, :, :], Aneg[:, :, :], ACT.Exp).then_inc(aneg_made, 1)
            act.wait_ge(aneg_made, 1)
            nc.scalar.activation(Aneg[:, :, :], Aneg[:, :, :], ACT.Copy, scale=-1.0).then_inc(aneg_made, 1)
            for p in FRONT0:
                if p == ("xp", 0):
                    for g in range(G - 2, G):
                        for _ in sigmoid(0, g, pro, "u"):
                            pass
                if p[0] == "M" and p[2] == 3:
                    row_rstd(0, p[1])
                for _ in evac(0, pro, p):
                    pass
                if p[0] == "u" and p[1] >= 2:
                    for _ in sigmoid(0, p[1] - 2, pro, "u"):
                        pass
            for g in range(HG):
                softplus(0, g)
            act.wait_ge(aneg_made, 2)
            opening(0, pro, True)
            with act.Fori(0, NCH - 1) as k:
                at = part(k)
                for s in range(CUT, SLOTS):
                    slot(k, s, mid_of(k, k + 1, at, s), steps_of(k, k + 1, at, s))
                opening(k + 1, at)
            k = NCH - 1
            at = part(k)
            for s in range(CUT, SLOTS):
                slot(k, s, mid_of(k, None, at, s), steps_of(k, None, at, s))

        @block.vector
        def _(dve):
            def read(at, job):
                b, n = at(job)
                dve.wait_ge(misc_ready[b], n + 1)
                return misc[b], misc_free[b], n + 1

            nc.vector.memset(state[:, :, :], 0.0).then_inc(state_saved, SLOTS)
            nc.vector.memset(tails[:, :, :], 0.0).then_inc(tails_saved, G)
            nc.vector.memset(mv[:, :, :], 0.0).then_inc(scan_done, SC)
            nc.vector.memset(rstd[:, :], 0.0).then_inc(stt_done, STC)
            dve.wait_ge(rows_in, 2 * 16)
            dve.wait_ge(w_quarter, 16)
            dve.wait_ge(w_first, 2 * 16)

            def half_of_bias(half):
                for a in range(half * G, half * G + G):
                    if a >= 2:
                        dve.wait_ge(bc_made, 2 * (a - 1))
                    nc.vector.tensor_tensor(products[a % 2], win[half][:, a % G, :], bf1, ALU.mult)\
                        .then_inc(bc_made, 1)
                    dve.wait_ge(bc_made, 2 * a + 1)
                    nc.vector.tensor_reduce(bc[:, a:a + 1], products[a % 2], mybir.AxisListType.X, ALU.add)\
                        .then_inc(bc_made, 1)

            half_of_bias(0)
            dve.wait_ge(x_in, 16)
            dve.wait_ge(scan_done, SC)
            for b in range(JB):
                if b >= 2:
                    dve.wait_ge(hid_chain, 2 * (b - 1))
                nc.vector.bn_stats(stats[:, b % 2, :], hid[:, b, :]).then_inc(hid_chain, 1)
                dve.wait_ge(hid_chain, 2 * b + 1)
                nc.vector.bn_aggr(mv[:, b, :], stats[:, b % 2, :]).then_inc(hid_chain, 1)
            dve.wait_ge(w_in, 4 * 16)
            half_of_bias(1)
            dve.wait_ge(rstd_step, 2)
            for b in range(JB):
                nc.vector.tensor_scalar(hid[:, b, :], hid[:, b, :], mv[:, b, 0:1], rstd[:, b:b + 1],
                                        ALU.subtract, ALU.mult).then_inc(hid_made, 1)
            for b in range(JB):
                dve.wait_ge(hid_made, b + 1)
                nc.vector.tensor_tensor(hid[:, b, :], hid[:, b, :], Wbc, ALU.mult).then_inc(hid_made, 1)
            dve.wait_ge(hid_made, 2 * JB)
            dve.wait_ge(ident_made, 2)
            dve.wait_ge(c_in, 6 * 16)
            dve.wait_ge(bc_made, 4 * G)
            nc.vector.tensor_tensor(bias_share[:, :], bc[:, 0:G], cw[:, :, KC - 1], ALU.mult).then_inc(diag_made, 1)
            dve.wait_ge(diag_made, 1)
            nc.vector.tensor_tensor(cb[:, :], cb[:, :], bias_share[:, :], ALU.add).then_inc(diag_made, 1)
            for g in range(G):
                nc.vector.tensor_scalar(diagD[:, g, :], ident[:, :], Dcol[:, g:g + 1], None, ALU.mult)\
                    .then_inc(diag_made, 1)

            def row_stats(c, at, i):
                b, n = at(("x1", i))
                ps, ready, free = misc[b], misc_ready[b], misc_free[b]
                r = i % 2
                base = (c * NB + i) * 2
                xr = x1new[:, i, :]

                def add():
                    dve.wait_ge(ready, n + 1)
                    dve.wait_ge(x_loaded, (c + 1) * 16)
                    nc.vector.tensor_tensor(xr, ps[:, 0:D], xr, ALU.add).then_inc(free, 1)

                def stats_of():
                    dve.wait_ge(free, n + 1)
                    wait(dve, ln_step, base - 2)
                    nc.vector.bn_stats(stats[:, r, :], xr).then_inc(ln_step, 1)

                def mean_of():
                    wait(dve, xn_made, c * NB + (i - 1))
                    wait(dve, pad_set, c * NB + i)
                    dve.wait_ge(ln_step, base + 1)
                    nc.vector.memset(pad[:, :], 0.0).then_inc(pad_set, 1)
                    nc.vector.bn_aggr(mv[:, r, :], stats[:, r, :]).then_inc(ln_step, 1)

                return [add, stats_of, mean_of]

            def normalize(c, at, i):
                r = i % 2
                xr = x1new[:, i, :]
                dve.wait_ge(rstd_step, (c * NB + i) * 2 + 4)
                if i < 2:
                    wait(dve, conv_step, c * G * (KC - 1))
                    dve.wait_ge(tails_saved, c * G + G)
                nc.vector.tensor_scalar(xn[i], xr, mv[:, r, 0:1], rstd[:, r:r + 1],
                                        ALU.subtract, ALU.mult).then_inc(xn_made, 1)
                dve.wait_ge(xn_made, c * NB + (i + 1))
                nc.vector.tensor_tensor(xr, xr, b2[:, :], ALU.add).then_inc(x1_made, 1)

            def conv(c, at, g):
                base = (c * G + g) * 3
                b, n = at(("u", g))
                src = upre[:, g % 2, :]

                def tap(t):
                    if t:
                        dve.wait_ge(conv_step, base + t)
                    else:
                        dve.wait_ge(misc_free[b], n + 1)
                        dve.wait_ge(upre_ready, (c * G + g) * 2 + 2)
                    nc.vector.scalar_tensor_tensor(u[:, g, :], src[:, 1 + t:1 + t + T], cw[:, g, t:t + 1],
                                                   u[:, g, :], ALU.mult, ALU.add).then_inc(conv_step, 1)

                return [lambda t=t: tap(t) for t in range(KC - 1)]

            def scan(k, s, j):
                n, g = s // 2, (s % 2) * HG + j
                q = k * 128 + (s * 4 + j)
                dve.wait_ge(dA_ready, q + 1)
                dve.wait_ge(dBu_ready, q + 1)
                if j == 0:
                    wait(dve, hT_ready, k * 128 + (s * 4 - 4))
                    dve.wait_ge(state_saved, k * SLOTS + (s + SLOTS - 1))
                nc.vector.tensor_tensor_scan(h[:, s % 2, j, :], dA[j % 2][:, :], dBu[:, j, :],
                                             state[:, n, g:g + 1], ALU.mult, ALU.add).then_inc(scan_done, 1)

            def save_state(k, s):
                dve.wait_ge(scan_done, k * 128 + (s * 4 + 4 + SC))
                half = s % 2
                nc.vector.tensor_copy(state[:, s // 2, half * HG:(half + 1) * HG], h[:, half, :, T - 1])\
                    .then_inc(state_saved, 1)

            def weigh(k, s, b, at):
                n, half = s // 2, s % 2
                dve.wait_ge(hT_ready, k * 128 + (s * 4 + b + 1))
                if s < 2:
                    bk, m = at(("uD", half * NB + b))
                    dve.wait_ge(misc_free[bk], m + 1)
                else:
                    dve.wait_ge(stt_done, k * 128 + ((s - 2) * 4 + b + 1 + STC))
                y = yT[:, b, half * T:(half + 1) * T]
                nc.vector.scalar_tensor_tensor(y, hT[b][:, :], Ct[:, b, n:n + 1], y, ALU.mult, ALU.add)\
                    .then_inc(stt_done, 1)

            def slot(k, s, at, items, early=()):
                early = list(early)
                items = [f if isinstance(f, list) else [f] for f in items]
                first = items.pop(0) if items else []
                second = items.pop(0) if items else []
                for j in range(HG):
                    if early:
                        early.pop(0)()
                    scan(k, s, j)
                    if j >= 1 and first:
                        first.pop(0)()
                save_state(k, s - 1)
                for b in range(NB):
                    weigh(k, s - 1, b, at)
                    if b >= 1 and second:
                        second.pop(0)()
                for steps in [first, second] + items:
                    for f in steps:
                        f()

            def front_items(k, c, at, s):
                if s == CUT + 1:
                    yield lambda: move_x1(k)
                for p in PLAN[s - 1]:
                    if p[0] == "u" and c is not None:
                        yield conv(c, at, p[1])
                for p in PLAN[s - 1]:
                    if p[0] == "M" and p[2] == 3 and c is not None:
                        yield lambda: None
                        yield lambda: None
                        yield lambda i=p[1]: normalize(c, at, i)
                if s == SLOTS - 2 and c is not None:
                    yield lambda: (cut(c, at, 0), cut(c, at, 1))
                if s == SLOTS - 1 and c is not None:
                    yield lambda: (cut(c, at, 2), cut(c, at, 3), top(c, 0))
                    for g in range(1, HG):
                        yield lambda g=g: top(c, g)

            def front_early(c, at, s):
                for p in PLAN[s - 1]:
                    if p[0] == "M" and p[2] == 3:
                        yield from row_stats(c, at, p[1])

            def close_scan(k, at_k):
                save_state(k, SLOTS - 1)
                for b in range(NB):
                    weigh(k, SLOTS - 1, b, at_k)

            def gate_y(k, at, g):
                ps, free, _ = read(at, ("y", g))
                dve.wait_ge(sig_used, z_item(k, g) + 1)
                nc.vector.tensor_tensor(gate[:, g, :], ps[:, :], gate[:, g, :], ALU.mult).then_inc(free, 1)

            def cut(c, at, g):
                b, n = at(("dt", g))
                dve.wait_ge(misc_free[b], n + 1)
                if g < HG:
                    dve.wait_ge(sig_used, u_item(c, G))
                else:
                    dve.wait_ge(delta_ready, c * G + (g - HG + 1))
                src = vdt if g < HG else delta
                nc.vector.tensor_scalar(tmp[:, g % 4, :], src[:, g, :], CLAMP, None, ALU.min)\
                    .then_inc(sp_clamped, 1)

            def top(c, g):
                dve.wait_ge(sp_step, (c * G + g) * 2 + 2)
                src = vdt if g < HG else delta
                if g < HG:
                    wait(dve, dBu_ready, c * 128 - HG)
                    wait(dve, dA_ready, c * 128 - HG)
                nc.vector.tensor_tensor(delta[:, g, :], src[:, g, :], tmp[:, g % 4, :], ALU.max)\
                    .then_inc(delta_ready, 1)

            def take_C(c, at):
                ps, free, n = read(at, ("ct", 0))
                dve.wait_ge(stt_done, c * 128 + STC)
                nc.vector.tensor_copy(Ct[:, :, :], ps[:, 0:NB * (R + 2 * NS)]
                                      .rearrange("p (b r) -> p b r", b=NB)[:, :, R + NS:]).then_inc(free, 1)
                dve.wait_ge(free, n)

            def opening(k, c, at):
                for g in range(HG, HG + 2):
                    cut(c, at, g)
                for j in range(2):
                    scan(c, 0, j)
                for g in range(HG + 2, G):
                    cut(c, at, g)
                take_C(c, at)
                scan(c, 0, 2)
                top(c, HG)
                scan(c, 0, 3)
                for g in range(G):
                    if 1 <= g < HG:
                        top(c, HG + g)
                    if k is not None:
                        gate_y(k, at, g)
                for s in range(1, CUT):
                    late = 0 <= s - 3 < NB and k is not None
                    slot(c, s, at, [lambda b=s - 3: finish(k, at, b)] if late else ())

            def finish(k, at, b):
                if b == 0:
                    dve.wait_ge(x1_moved, k + 1)
                ps, free, _ = read(at, ("o", b))
                nc.vector.tensor_tensor(x1cur[:, b, :], ps[:, 0:D], x1cur[:, b, :], ALU.add).then_inc(free, 1)

            def move_x1(k):
                dve.wait_ge(x1_made, (k + 1) * NB)
                wait(dve, out_stored, k * 16)
                nc.vector.tensor_copy(x1cur[:, :, :], x1new[:, :, :]).then_inc(x1_moved, 1)

            pro = part(None)
            for p in FRONT0:
                if p[0] == "u":
                    g = p[1]
                    for f in conv(0, pro, g):
                        f()
                    dve.wait_ge(conv_step, g * 3 + 3)
                    wait(dve, sig_used, g - 3)
                    nc.vector.tensor_scalar(tmp[:, g % 4, :], u[:, g, :], SCLAMP, 0.0, ALU.add, ALU.max)\
                        .then_inc(relu_made, 1)
                elif p[0] == "M" and p[2] == 3:
                    for f in row_stats(0, pro, p[1]):
                        f()
                    normalize(0, pro, p[1])
            for g in range(HG):
                cut(0, pro, g)
            for g in range(HG):
                top(0, g)
            opening(None, 0, pro)
            with dve.Fori(0, NCH - 1) as k:
                at = part(k)
                for s in range(CUT, SLOTS):
                    slot(k, s, at, front_items(k, k + 1, at, s), front_early(k + 1, at, s))
                close_scan(k, at)
                opening(k, k + 1, at)
            k = NCH - 1
            at = part(k)
            for s in range(CUT, SLOTS):
                slot(k, s, at, front_items(k, None, at, s))
            close_scan(k, at)
            for g in range(G):
                gate_y(k, at, g)
            for b in range(NB):
                finish(k, at, b)

        @block.tensor
        def _(pe):
            def bank(at, job):
                b, n = at(job)
                wait(pe, misc_free[b], n)
                return misc[b], misc_ready[b]

            def turn(dst, src):
                k_, m_ = src.shape[0], src.shape[1]
                return nc.tensor.transpose(dst, src, ident[0:k_, 0:k_])

            def piece(c, at, p):
                if p[0] == "T":
                    ps, ready = bank(at, p)
                    _, i, q = p
                    pe.wait_ge(adj_loaded[q // 2], (c * NB + i + 1) * 16)
                    for a in range(4):
                        col = (q % 2) * T + a * P
                        last = turn(ps[:, a * P:(a + 1) * P], adj_in[:, q // 2, col:col + P])
                    last.then_inc(ready, 1)
                elif p[0] == "M":
                    _, i, q = p
                    b, n = at(("x1", i))
                    if q == 0:
                        wait(pe, misc_free[b], n)
                    bt, nt = at(("T", i, q))
                    pe.wait_ge(misc_free[bt], nt + 1)
                    for a in range(4):
                        last = nc.tensor.matmul(misc[b][:, 0:D], adjT[:, q % 2, a, :], hid[:, q * 4 + a, :],
                                                start=(q == 0 and a == 0), stop=(q == 3 and a == 3))
                    if q == 3:
                        last.then_inc(misc_ready[b], 1)
                elif p[0] == "xn":
                    i = p[1]
                    ps, ready = bank(at, p)
                    pe.wait_ge(xn_made, c * NB + i + 1)
                    for a in range(2):
                        last = turn(ps[:, a * P:(a + 1) * P], xn[i][:, a * P:(a + 1) * P])
                    last.then_inc(ready, 1)
                elif p[0] in ("z", "u"):
                    g = p[1]
                    ps, ready = bank(at, p)
                    if p[0] == "u" and g == 0:
                        b, n = at(("xn", NB - 1))
                        pe.wait_ge(misc_free[b], n + 1)
                    col = (DI if p[0] == "z" else 0) + g * P
                    for a in range(2):
                        last = nc.tensor.matmul(ps[:, :], WcT[:, a, col:col + P], xnT[:, a, :],
                                                start=(a == 0), stop=(a == 1))
                    last.then_inc(ready, 1)
                elif p[0] == "xp":
                    g = p[1]
                    b, n = at(("xp",))
                    if g == 0:
                        wait(pe, misc_free[b], n)
                    pe.wait_ge(sig_used, u_item(c, g) + 1)
                    last = nc.tensor.matmul(misc[b][0:R + 2 * NS, :], WxT[:, g, :], u[:, g, :],
                                            start=(g == 0), stop=(g == G - 1))
                    if g == G - 1:
                        last.then_inc(misc_ready[b], 1)
                elif p[0] == "dt":
                    if p[1] == 0:
                        b, n = at(("xp",))
                        pe.wait_ge(misc_free[b], n + 1)
                    dt_job(at, p[1])

            def turn_h(k, s):
                half = s % 2
                pe.wait_ge(scan_done, k * 128 + (s * 4 + 4 + SC))
                for b in range(NB):
                    pe.wait_ge(stt_done, k * 128 + (s * 4 + b - 3 + STC))
                    for j in range(HG):
                        last = turn(hT[b][:, j * P:(j + 1) * P], h[:, half, j, b * P:(b + 1) * P])
                    last.then_inc(hT_ready, 1)

            def dt_job(at, g):
                ps, ready = bank(at, ("dt", g))
                nc.tensor.matmul(ps[:, :], WdtT[:, g * P:(g + 1) * P], dbc[0:R, :], start=True, stop=True)\
                    .then_inc(ready, 1)

            def y_job(at, g):
                ps, ready = bank(at, ("y", g))
                for b in range(NB):
                    last = turn(ps[:, b * P:(b + 1) * P], yT[:, b, g * P:(g + 1) * P])
                last.then_inc(ready, 1)

            def y_jobs(k, at):
                for g in range(G):
                    if g % HG == 0:
                        pe.wait_ge(stt_done, k * 128 + (128 - HG + g + STC))
                    y_job(at, g)

            def out_job(at, b):
                ps, ready = bank(at, ("o", b))
                for g in range(G):
                    last = nc.tensor.matmul(ps[:, 0:D], gate[:, g, b * P:(b + 1) * P], WocT[:, g, :],
                                            start=(g == 0), stop=(g == G - 1))
                last.then_inc(ready, 1)

            def boundary(k, c, at):
                if k is not None:
                    turn_h(k, SLOTS - 1)
                for g in range(HG + 2, G):
                    dt_job(at, g)
                ps, ready = bank(at, ("ct", 0))
                w = R + 2 * NS
                for b in range(NB):
                    last = nc.tensor.matmul(ps[:, b * w:(b + 1) * w], dbc[:, b * P:(b + 1) * P],
                                            ident[0:w, 0:w], start=True, stop=True)
                last.then_inc(ready, 1)
                if k is not None:
                    y_jobs(k, at)
                for j in range(2 * NB):
                    if j == NB:
                        turn_h(c, 0)
                    ps, ready = bank(at, ("uD", j))
                    b = j % NB
                    for a in range(HG):
                        g = (j // NB) * HG + a
                        last = nc.tensor.matmul(ps[:, a * P:(a + 1) * P], u[:, g, b * P:(b + 1) * P],
                                                diagD[:, g, :], start=True, stop=True)
                    last.then_inc(ready, 1)

            pro = part(None)
            pe.wait_ge(ident_made, 2)

            def half_of_W_in(half):
                for a in range(half * 8, half * 8 + 8):
                    ps, ready = bank(pro, ("wi", a))
                    eb, mb = a // 4, a % 4
                    if a == 4:
                        pe.wait_ge(w_first, 2 * 16)
                    for e in range(4):
                        row = eb * 4 + e
                        last = turn(ps[:, e * P:(e + 1) * P], win[row // 8][:, row % 8, mb * P:(mb + 1) * P])
                    last.then_inc(ready, 1)

            def half_of_product(half):
                for a in range(2):
                    b, n = pro(("wi", half * 8 + 6 + a))
                    pe.wait_ge(misc_free[b], n + 1)
                for a in range(half * 4, half * 4 + 4):
                    ps, ready = bank(pro, ("wc", a))
                    eb, ib = a // 2, a % 2
                    for mb in range(4):
                        last = nc.tensor.matmul(ps[:, :], wfc1[:, mb, ib * P:(ib + 1) * P],
                                                winT[mb // 2][:, mb % 2, eb * T:(eb + 1) * T],
                                                start=(mb == 0), stop=(mb == 3))
                    last.then_inc(ready, 1)

            pe.wait_ge(w_quarter, 16)
            half_of_W_in(0)
            half_of_product(0)
            pe.wait_ge(w_in, 4 * 16)
            half_of_W_in(1)
            for a in range(2):
                ps, ready = bank(pro, ("wf", a))
                for e in range(4):
                    mb, ob = 2 * a + e // 2, e % 2
                    last = turn(ps[:, e * P:(e + 1) * P], wfc2[:, ob, mb * P:(mb + 1) * P])
                last.then_inc(ready, 1)
            ps, ready = bank(pro, ("wx", 0))
            w = R + 2 * NS
            for g in range(G):
                last = turn(ps[:, g * w:(g + 1) * w], wxp[:, g * P:(g + 1) * P])
            last.then_inc(ready, 1)
            for a in range(2):
                ps, ready = bank(pro, ("wd", a))
                for e in range(4):
                    last = nc.tensor.matmul(ps[0:R, e * P:(e + 1) * P], wdt[:, a * 4 + e, :], ident[:, :],
                                            start=True, stop=True)
                last.then_inc(ready, 1)
            half_of_product(1)
            pe.wait_ge(hid_made, 2 * JB)
            for p in FRONT0:
                if p[0] == "u" and p[1] == 0:
                    for name in (("wc", 7), ("wc", 6)):
                        b, n = pro(name)
                        pe.wait_ge(misc_free[b], n + 1)
                piece(0, pro, p)
            pe.wait_ge(diag_made, G + 2)
            boundary(None, 0, pro)
            for s in range(2, CUT):
                turn_h(0, s - 1)
                if s == 2:
                    pe.wait_ge(w_out, 16)
                if s - 2 < 4:
                    a = s - 2
                    ps, ready = bank(pro, ("wo", a))
                    for e in range(2):
                        g = 2 * a + e
                        for mb in range(4):
                            last = nc.tensor.matmul(ps[:, e * D:(e + 1) * D], wout[:, mb, g * P:(g + 1) * P],
                                                    wfc2T[:, mb, :], start=(mb == 0), stop=(mb == 3))
                    last.then_inc(ready, 1)
            with pe.Fori(0, NCH - 1) as k:
                at = part(k)
                for s in range(CUT, SLOTS):
                    turn_h(k, s - 1)
                    for p in PLAN[s]:
                        piece(k + 1, at, p)
                boundary(k, k + 1, at)
                for s in range(1, CUT):
                    if s > 1:
                        turn_h(k + 1, s - 1)
                    if 0 <= s - 2 < NB:
                        out_job(at, s - 2)
            k = NCH - 1
            at = part(k)
            for s in range(CUT, SLOTS):
                turn_h(k, s - 1)
                for p in PLAN[s]:
                    if p[0] == "z":
                        piece(None, at, p)
            turn_h(k, SLOTS - 1)
            y_jobs(k, at)
            b, n = at(("y", G - 1))
            pe.wait_ge(misc_free[b], n + 1)
            for b in range(NB):
                out_job(at, b)


_INS = ['x', 'adj', 'L0_gnn_W', 'L0_ffn_W_fc1', 'L0_ffn_b_fc1', 'L0_ffn_W_in', 'L0_ffn_conv_w', 'L0_ffn_conv_b',
        'L0_ffn_W_xproj', 'L0_ffn_W_dt', 'L0_ffn_b_dt', 'L0_ffn_A_log', 'L0_ffn_D', 'L0_ffn_W_out',
        'L0_ffn_W_fc2', 'L0_ffn_b_fc2']


def kernel(**inputs):
    import numpy as _np
    import concourse.bacc as _bacc
    from concourse import mybir as _mybir
    from concourse.bass_utils import run_bass_kernel_spmd as _run

    nc = _bacc.Bacc("TRN2", target_bir_lowering=False, num_devices=1)
    arrays, args = {}, []
    for name in _INS:
        a = _np.ascontiguousarray(inputs[name])
        arrays[f"in_{name}"] = a
        args.append(nc.dram_tensor(f"in_{name}", a.shape, _mybir.dt.from_np(a.dtype), kind="ExternalInput").ap())
    args.append(nc.dram_tensor("out_0", (N, D), _mybir.dt.float32, kind="ExternalOutput").ap())
    build(nc, *args)
    r = _run(nc, [arrays], core_ids=[0])
    return r.results[0]["out_0"]
```
